# Optimizing a Trainium2 kernel written in Bass

```python
import numpy as np
import jax
import jax.numpy as jnp

def _softmax(x, axis=-1):
    return jax.nn.softmax(x, axis=axis)

def _gelu(x):
    return jax.nn.gelu(x, approximate=True)

def _silu(x):
    return jax.nn.silu(x)

def _sigmoid(x):
    return jax.nn.sigmoid(x)

def _layernorm(x, axis=-1, eps=1e-05):
    m = jnp.mean(x, axis=axis, keepdims=True)
    v = jnp.var(x, axis=axis, keepdims=True)
    return (x - m) / jnp.sqrt(v + eps)

def _scatter_add(tgt, idx, src, axis=0):
    return tgt.at[idx].add(src)

def _segment_sum(src, seg, n):
    return jax.ops.segment_sum(src, seg, n)
kernel_name = 'mk_conv_seq_d2_conv_nhwc512_r4_1bac5c'

def setup_inputs(seed: int=0):
    np.random.seed(seed)
    _w = jnp.asarray

    def _rec_inputs():
        import jax
        import jax.numpy as jnp
        _gk = jax.random.key(seed)
        x = 7.22e-05 + 1 * jax.random.normal(jax.random.fold_in(_gk, 1), (4, 16, 16, 128), jnp.float32)
        return x
    x = _rec_inputs()

    def _L0_conv_setup():
        import jax, jax.numpy as jnp
        import numpy as np
        B, H, W, C = (4, 16, 16, 128)
        R, NH, KS = (2, 8, 7)
        S = 1.0

        def layernorm(t, g, b):
            m = t.mean(-1, keepdims=True)
            v = ((t - m) ** 2).mean(-1, keepdims=True)
            return (t - m) / jnp.sqrt(v + 1e-05) * g + b

        def grid_sample_bilinear_zeros(img, grid):
            b, c, h, w = img.shape
            gh, gw = (grid.shape[1], grid.shape[2])
            x = (grid[..., 0] + 1.0) * 0.5 * (w - 1)
            y = (grid[..., 1] + 1.0) * 0.5 * (h - 1)
            x0 = jnp.floor(x)
            y0 = jnp.floor(y)
            wx1 = x - x0
            wy1 = y - y0
            x0i = x0.astype(jnp.int32)
            y0i = y0.astype(jnp.int32)
            flat = img.reshape(b, c, h * w)

            def corner(xi, yi, wt):
                valid = ((xi >= 0) & (xi < w) & (yi >= 0) & (yi < h)).astype(img.dtype)
                idx = jnp.clip(yi, 0, h - 1) * w + jnp.clip(xi, 0, w - 1)
                vals = jnp.take_along_axis(flat, idx.reshape(b, 1, gh * gw), axis=2)
                return vals * (valid * wt).reshape(b, 1, gh * gw)
            out = corner(x0i, y0i, (1 - wx1) * (1 - wy1)) + corner(x0i + 1, y0i, wx1 * (1 - wy1)) + corner(x0i, y0i + 1, (1 - wx1) * wy1) + corner(x0i + 1, y0i + 1, wx1 * wy1)
            return out.reshape(b, c, gh, gw)
        key = jax.random.key(seed)
        ks = jax.random.split(key, 12)
        sd = 0.02
        f32 = jnp.float32
        return {'x': jax.random.normal(ks[0], (B, H, W, C), f32), 'ln_g': jnp.ones((C,), f32), 'ln_b': jnp.zeros((C,), f32), 'wq': jax.random.normal(ks[1], (C, C), f32) * sd, 'bq': jnp.zeros((C,), f32), 'wv': jax.random.normal(ks[2], (C, C), f32) * sd, 'bv': jnp.zeros((C,), f32), 'dw_w': jax.random.normal(ks[3], (C, 1, KS, KS), f32) * sd, 'dw_b': jnp.zeros((C,), f32), 'pw_w': jax.random.normal(ks[4], (2, C, 1, 1), f32) * sd, 'mq_w': jax.random.normal(ks[5], (C, C), f32) * sd, 'mq_b': jnp.zeros((C,), f32), 'mk_w': jax.random.normal(ks[6], (C, C), f32) * sd, 'mk_b': jnp.zeros((C,), f32), 'mv_w': jax.random.normal(ks[7], (C, C), f32) * sd, 'mv_b': jnp.zeros((C,), f32), 'mo_w': jax.random.normal(ks[8], (C, C), f32) * sd, 'mo_b': jnp.zeros((C,), f32), 'mlp_w': jax.random.normal(ks[9], (C, C), f32) * sd, 'mlp_b': jnp.zeros((C,), f32)}
    _L0_conv_all = _L0_conv_setup()
    _L0_conv_in = {k: v for k, v in _L0_conv_all.items() if k in ('ln_g', 'ln_b', 'wq', 'bq', 'wv', 'bv', 'dw_w', 'dw_b', 'pw_w', 'mq_w', 'mq_b', 'mk_w', 'mk_b', 'mv_w', 'mv_b', 'mo_w', 'mo_b', 'mlp_w', 'mlp_b')}
    del _L0_conv_all

    def _L1_conv_setup():
        import jax, jax.numpy as jnp
        import numpy as np
        GROUPS = 32
        EPS = 1e-06
        key = jax.random.key(seed)
        ks = jax.random.split(key, 6)
        B, H, W, C = (4, 16, 16, 128)
        s = 1.0 / np.sqrt(C)
        return {'inputs': jax.random.normal(ks[0], (B, H, W, C), dtype=jnp.float32), 'gn_gamma': jnp.ones((C,), dtype=jnp.float32), 'gn_beta': jnp.zeros((C,), dtype=jnp.float32), 'wq': jax.random.normal(ks[1], (C, C), dtype=jnp.float32) * s, 'bq': jnp.zeros((C,), dtype=jnp.float32), 'wk': jax.random.normal(ks[2], (C, C), dtype=jnp.float32) * s, 'bk': jnp.zeros((C,), dtype=jnp.float32), 'wv': jax.random.normal(ks[3], (C, C), dtype=jnp.float32) * s, 'bv': jnp.zeros((C,), dtype=jnp.float32), 'wo': jax.random.normal(ks[4], (C, C), dtype=jnp.float32) * s, 'bo': jnp.zeros((C,), dtype=jnp.float32)}
    _L1_conv_all = _L1_conv_setup()
    _L1_conv_in = {k: v for k, v in _L1_conv_all.items() if k in ('gn_gamma', 'gn_beta', 'wq', 'bq', 'wk', 'bk', 'wv', 'bv', 'wo', 'bo')}
    del _L1_conv_all
    return {'x': x, 'L0_conv_ln_g': _L0_conv_in['ln_g'], 'L0_conv_ln_b': _L0_conv_in['ln_b'], 'L0_conv_wq': _L0_conv_in['wq'], 'L0_conv_bq': _L0_conv_in['bq'], 'L0_conv_wv': _L0_conv_in['wv'], 'L0_conv_bv': _L0_conv_in['bv'], 'L0_conv_dw_w': _L0_conv_in['dw_w'], 'L0_conv_dw_b': _L0_conv_in['dw_b'], 'L0_conv_pw_w': _L0_conv_in['pw_w'], 'L0_conv_mq_w': _L0_conv_in['mq_w'], 'L0_conv_mq_b': _L0_conv_in['mq_b'], 'L0_conv_mk_w': _L0_conv_in['mk_w'], 'L0_conv_mk_b': _L0_conv_in['mk_b'], 'L0_conv_mv_w': _L0_conv_in['mv_w'], 'L0_conv_mv_b': _L0_conv_in['mv_b'], 'L0_conv_mo_w': _L0_conv_in['mo_w'], 'L0_conv_mo_b': _L0_conv_in['mo_b'], 'L0_conv_mlp_w': _L0_conv_in['mlp_w'], 'L0_conv_mlp_b': _L0_conv_in['mlp_b'], 'L1_conv_gn_gamma': _L1_conv_in['gn_gamma'], 'L1_conv_gn_beta': _L1_conv_in['gn_beta'], 'L1_conv_wq': _L1_conv_in['wq'], 'L1_conv_bq': _L1_conv_in['bq'], 'L1_conv_wk': _L1_conv_in['wk'], 'L1_conv_bk': _L1_conv_in['bk'], 'L1_conv_wv': _L1_conv_in['wv'], 'L1_conv_bv': _L1_conv_in['bv'], 'L1_conv_wo': _L1_conv_in['wo'], 'L1_conv_bo': _L1_conv_in['bo']}

def reference(x, L0_conv_ln_g, L0_conv_ln_b, L0_conv_wq, L0_conv_bq, L0_conv_wv, L0_conv_bv, L0_conv_dw_w, L0_conv_dw_b, L0_conv_pw_w, L0_conv_mq_w, L0_conv_mq_b, L0_conv_mk_w, L0_conv_mk_b, L0_conv_mv_w, L0_conv_mv_b, L0_conv_mo_w, L0_conv_mo_b, L0_conv_mlp_w, L0_conv_mlp_b, L1_conv_gn_gamma, L1_conv_gn_beta, L1_conv_wq, L1_conv_bq, L1_conv_wk, L1_conv_bk, L1_conv_wv, L1_conv_bv, L1_conv_wo, L1_conv_bo):
    import jax
    import jax.numpy as jnp

    def _L0_conv_ref(x, ln_g, ln_b, wq, bq, wv, bv, dw_w, dw_b, pw_w, mq_w, mq_b, mk_w, mk_b, mv_w, mv_b, mo_w, mo_b, mlp_w, mlp_b):
        import jax, jax.numpy as jnp
        import numpy as np
        B, H, W, C = (4, 16, 16, 128)
        R, NH, KS = (2, 8, 7)
        S = 1.0

        def layernorm(t, g, b):
            m = t.mean(-1, keepdims=True)
            v = ((t - m) ** 2).mean(-1, keepdims=True)
            return (t - m) / jnp.sqrt(v + 1e-05) * g + b

        def grid_sample_bilinear_zeros(img, grid):
            b, c, h, w = img.shape
            gh, gw = (grid.shape[1], grid.shape[2])
            x = (grid[..., 0] + 1.0) * 0.5 * (w - 1)
            y = (grid[..., 1] + 1.0) * 0.5 * (h - 1)
            x0 = jnp.floor(x)
            y0 = jnp.floor(y)
            wx1 = x - x0
            wy1 = y - y0
            x0i = x0.astype(jnp.int32)
            y0i = y0.astype(jnp.int32)
            flat = img.reshape(b, c, h * w)

            def corner(xi, yi, wt):
                valid = ((xi >= 0) & (xi < w) & (yi >= 0) & (yi < h)).astype(img.dtype)
                idx = jnp.clip(yi, 0, h - 1) * w + jnp.clip(xi, 0, w - 1)
                vals = jnp.take_along_axis(flat, idx.reshape(b, 1, gh * gw), axis=2)
                return vals * (valid * wt).reshape(b, 1, gh * gw)
            out = corner(x0i, y0i, (1 - wx1) * (1 - wy1)) + corner(x0i + 1, y0i, wx1 * (1 - wy1)) + corner(x0i, y0i + 1, (1 - wx1) * wy1) + corner(x0i + 1, y0i + 1, wx1 * wy1)
            return out.reshape(b, c, gh, gw)
        b, h, w, c = x.shape
        x_ln = layernorm(x, ln_g, ln_b).transpose(0, 3, 1, 2)
        x_flat = x_ln.reshape(b, h * w, c)
        q = x_flat @ wq + bq
        q_img = q.reshape(b, c, h, w)
        o = jax.lax.conv_general_dilated(q_img, dw_w, (R, R), [(KS // 2, KS // 2)] * 2, dimension_numbers=('NCHW', 'OIHW', 'NCHW'), feature_group_count=c)
        o = jax.nn.gelu(o + dw_b[None, :, None, None], approximate=False)
        offsets = jax.lax.conv_general_dilated(o, pw_w, (1, 1), [(0, 0), (0, 0)], dimension_numbers=('NCHW', 'OIHW', 'NCHW'))
        hg, wg = (offsets.shape[2], offsets.shape[3])
        ref_x = (jnp.arange(wg, dtype=x.dtype) + 0.5) * (2.0 / wg) - 1.0
        ref_y = (jnp.arange(hg, dtype=x.dtype) + 0.5) * (2.0 / hg) - 1.0
        gx, gy = jnp.meshgrid(ref_x, ref_y, indexing='ij')
        refs = jnp.stack([gx, gy], axis=0)
        deformed = refs[None] + S * jnp.tanh(offsets)
        deformed = (deformed + 1.0) * (h / R) / 2.0
        grid = deformed[:, ::-1].transpose(0, 2, 3, 1)
        interp = grid_sample_bilinear_zeros(x.transpose(0, 3, 1, 2), grid)
        interp_flat = interp.reshape(b, hg * wg, c)
        v = interp_flat @ wv + bv
        k = interp_flat @ wv + bv
        hd = c // NH

        def heads(t):
            return t.reshape(b, -1, NH, hd).transpose(0, 2, 1, 3)
        qh = heads(q @ mq_w + mq_b)
        kh = heads(k @ mk_w + mk_b)
        vh = heads(v @ mv_w + mv_b)
        attn = jax.nn.softmax(jnp.einsum('bnqd,bnkd->bnqk', qh, kh), axis=-1)
        att = jnp.einsum('bnqk,bnkd->bnqd', attn, vh).transpose(0, 2, 1, 3).reshape(b, h * w, c)
        msa = att @ mo_w + mo_b
        z = msa + x.reshape(b, h * w, c)
        z_ln = layernorm(z, ln_g, ln_b)
        out = jax.nn.gelu(z_ln @ mlp_w + mlp_b, approximate=False) + z
        return out.reshape(b, w, h, c)

    def _L1_conv_ref(inputs, gn_gamma, gn_beta, wq, bq, wk, bk, wv, bv, wo, bo):
        import jax, jax.numpy as jnp
        import numpy as np
        GROUPS = 32
        EPS = 1e-06
        B, H, W, C = inputs.shape
        xg = inputs.astype(jnp.float32).reshape(B, H, W, GROUPS, C // GROUPS)
        mean = jnp.mean(xg, axis=(1, 2, 4), keepdims=True)
        var = jnp.var(xg, axis=(1, 2, 4), keepdims=True)
        xg = (xg - mean) * jax.lax.rsqrt(var + EPS)
        x = xg.reshape(B, H, W, C) * gn_gamma + gn_beta
        q = jnp.einsum('bhwc,cd->bhwd', x, wq) + bq
        k = jnp.einsum('bhwc,cd->bhwd', x, wk) + bk
        v = jnp.einsum('bhwc,cd->bhwd', x, wv) + bv
        N = H * W
        q = q.reshape(B, N, C) * (1.0 / jnp.sqrt(jnp.float32(C)))
        k = k.reshape(B, N, C)
        v = v.reshape(B, N, C)
        scores = jnp.einsum('bnc,bmc->bnm', q, k)
        attn = jax.nn.softmax(scores.astype(jnp.float32), axis=-1).astype(q.dtype)
        out = jnp.einsum('bmc,bnm->bnc', v, attn)
        out = out.reshape(B, H, W, C)
        out = jnp.einsum('bhwc,cd->bhwd', out, wo) + bo
        return out + inputs

    def _gn(v, G=32, eps=1e-05):
        B_, H_, W_, C_ = v.shape
        g = v.reshape(B_, H_, W_, G, C_ // G)
        m = jnp.mean(g, axis=(1, 2, 4), keepdims=True)
        s = jnp.var(g, axis=(1, 2, 4), keepdims=True)
        return ((g - m) / jnp.sqrt(s + eps)).reshape(v.shape)

    def _ln_c(v, eps=1e-06):
        m = jnp.mean(v, axis=-1, keepdims=True)
        s = jnp.var(v, axis=-1, keepdims=True)
        return (v - m) / jnp.sqrt(s + eps)

    def _ln_t(v, eps=1e-05):
        m = jnp.mean(v, axis=-1, keepdims=True)
        s = jnp.var(v, axis=-1, keepdims=True)
        return (v - m) / jnp.sqrt(s + eps)

    def _to_tokens(v):
        B_, H_, W_, C_ = v.shape
        return v.reshape(B_, H_ * W_, C_)

    def _from_tokens(t, like):
        return t.reshape(like.shape)
    x = _L0_conv_ref(x, L0_conv_ln_g, L0_conv_ln_b, L0_conv_wq, L0_conv_bq, L0_conv_wv, L0_conv_bv, L0_conv_dw_w, L0_conv_dw_b, L0_conv_pw_w, L0_conv_mq_w, L0_conv_mq_b, L0_conv_mk_w, L0_conv_mk_b, L0_conv_mv_w, L0_conv_mv_b, L0_conv_mo_w, L0_conv_mo_b, L0_conv_mlp_w, L0_conv_mlp_b)
    x = _L1_conv_ref(x, L1_conv_gn_gamma, L1_conv_gn_beta, L1_conv_wq, L1_conv_bq, L1_conv_wk, L1_conv_bk, L1_conv_wv, L1_conv_bv, L1_conv_wo, L1_conv_bo)
    return x

_drawn_inputs = setup_inputs


def setup_inputs(seed=0):
    import zlib

    import numpy as np

    out = dict(_drawn_inputs(seed))
    spreads = {'L0_conv_ln_g': (1.0, 0.572),
     'L0_conv_ln_b': (0.0, 0.538),
     'L0_conv_bq': (0.0, 0.8),
     'L0_conv_bv': (0.0, 0.8),
     'L0_conv_dw_b': (0.0, 0.8),
     'L0_conv_mq_b': (0.0, 0.8),
     'L0_conv_mk_b': (0.0, 0.8),
     'L0_conv_mv_b': (0.0, 0.278),
     'L0_conv_mo_b': (0.0, 0.1),
     'L0_conv_mlp_b': (0.0, 0.1),
     'L1_conv_gn_gamma': (1.0, 0.2),
     'L1_conv_gn_beta': (0.0, 0.1),
     'L1_conv_bq': (0.0, 0.492),
     'L1_conv_bk': (0.0, 0.8),
     'L1_conv_bv': (0.0, 0.1),
     'L1_conv_bo': (0.0, 0.1)}
    factors = {'L0_conv_wq': 8.0,
     'L0_conv_wv': 8.0,
     'L0_conv_dw_w': 8.0,
     'L0_conv_pw_w': 8.0,
     'L0_conv_mq_w': 8.0,
     'L0_conv_mk_w': 8.0,
     'L0_conv_mv_w': 8.0}
    for name, (base, spread) in spreads.items():
        noise = np.random.default_rng([zlib.crc32(name.encode()), seed]).standard_normal(out[name].shape)
        drawn = base * np.exp(spread * noise) if base else spread * noise
        out[name] = jnp.asarray(drawn.astype(out[name].dtype))
    for name, factor in factors.items():
        out[name] = (out[name] * factor).astype(out[name].dtype)
    return out
```

```python
from contextlib import ExitStack

import concourse.bass as bass
from concourse import mybir
from concourse.alu_op_type import AluOpType as ALU

F32 = mybir.dt.float32
ACT = mybir.ActivationFunctionType
AX = mybir.AxisListType

P = 128
B, H, W, C = 4, 16, 16, 128
HW = H * W
S = HW // P
T = B * S
NH = 8
HD = C // NH
PAIRS = NH // 2
KS, R = 7, 2
OH, OW = H // R, W // R
PIX = OH * OW
VW = 2 * HD + 2
LN_EPS, GN_EPS = 1e-5, 1e-6
GROUP = C // 32

SMALL = [("ident", P), ("dw_w", KS * KS), ("pw", 2), ("dw_b", 1), ("bq", 1), ("mq_b", 1), ("bv", 1), ("mk_b", 1),
         ("mv_b", 1), ("ln_g", 1), ("ln_b", 1), ("gn_gamma", 1), ("gn_beta", 1), ("bq1", 1), ("bk1", 1), ("bv1", 1),
         ("head_of", NH), ("ones_mask", 2), ("grid_x", PIX), ("grid_y", S * PIX),
         ("group_mean", P)]
LARGE = [("wq_conv", C), ("wqT", C), ("mq_w", C), ("wvT", C), ("mk_w", C), ("mv_w", C), ("mo_w", C), ("mlp_w", C),
         ("wv1T", C), ("wo1", C), ("wq1", C), ("wk1", C)]
ROWS = ["bq_conv", "mo_b", "mlp_b", "bo1"]


def columns(parts):
    at, out = 0, {}
    for name, n in parts:
        out[name] = (at, at + n)
        at += n
    return out, at


SMALL_AT, SMALL_N = columns(SMALL)
LARGE_AT, LARGE_N = columns(LARGE)


def tap_range(k, n):
    shift, phase = divmod(k - KS // 2, R)
    return phase, shift, max(0, -shift), min(n, n - shift)


def build(nc, x, small, large, rows, ln_rows, out):
    ctx = ExitStack()
    with ctx:
        def sb(name, shape, dt=F32):
            return ctx.enter_context(nc.sbuf_tensor(name, shape, dt))

        def sem(name):
            return ctx.enter_context(nc.semaphore(name))

        bank = [ctx.enter_context(nc.psum_tensor(f"bank{i}", [P, 512], F32)) for i in range(8)]

        x_hw = sb("x_hw", [P, T, C])
        x_st = sb("x_st", [P, B, S * C])
        sm = sb("sm", [P, SMALL_N])
        lg = sb("lg", [P, LARGE_N])
        row = sb("row", [1, len(ROWS) * C])
        gb = sb("gb", [P, 2 * C])
        ones_row = sb("ones_row", [1, P])
        eps = sb("eps", [P, 2])
        neg_half = sb("neg_half", [P, 2 * B])

        def w(name):
            if name in SMALL_AT:
                a, b = SMALL_AT[name]
                return sm[:, a:b]
            a, b = LARGE_AT[name]
            return lg[:, a:b]

        def r(name):
            i = ROWS.index(name)
            return row[:, i * C:(i + 1) * C]

        st = sb("st", [P, T, 6])
        mv = sb("mv", [P, T, 2])
        sd = sb("sd", [P, T])
        rstd = sb("rstd", [P, T])
        nmr = sb("nmr", [P, T])
        x_hat = sb("x_hat", [P, T, C])
        x_g = sb("x_g", [P, T, C])
        x_ln = sb("x_ln", [P, T, C])
        m_q = sb("m_q", [P, C])
        m_kv = sb("m_kv", [P, 2 * C])
        w_vo = sb("w_vo", [P, C])
        cols = sb("cols", [P, 3])
        msa_bias = sb("msa_bias", [P, C])
        out_bias = sb("out_bias", [P, C])
        x_res = sb("x_res", [P, T, C])
        diag = sb("diag", [P, KS * KS, P])
        q_conv = sb("q_conv", [P, 2 * OH * B * 2 * OW])
        acc = sb("acc", [P, OH * B * OW])
        conv_sum = sb("conv_sum", [P, OH * B * OW])
        o_act = sb("o_act", [P, B, OH, OW])
        qh = sb("qh", [P, T * P])
        tanh = sb("tanh", [P, 2, B * PIX])
        dist_x = sb("dist_x", [P, B, PIX])
        dist_y = sb("dist_y", [P, S, B, PIX])
        falling_x = sb("falling_x", [P, B * PIX])
        abs_y = sb("abs_y", [P, S * B * PIX])
        hat_x = sb("hat_x", [P, B * PIX])
        hat_y = sb("hat_y", [P, S, B * PIX])
        bilin = sb("bilin", [P, S, B, PIX])
        sampled = sb("sampled", [P, B, PIX])
        k_t = sb("k_t", [P, B, PIX])
        k_blk = sb("k_blk", [P, B, NH, PIX])
        v_blk = sb("v_blk", [P, B, PAIRS, VW])
        smax = sb("smax", [P, 2, NH])
        s_sub = sb("s_sub", [P, 2, NH, PIX])
        p_t = sb("p_t", [P, 2, PAIRS, P])
        recip = sb("recip", [P, 2, NH])
        att = sb("att", [P, 2, C])
        att_t = sb("att_t", [P, 2, P])
        z = sb("z", [P, T, C])
        zst = sb("zst", [P, T, 6])
        zmv = sb("zmv", [P, T, 2])
        zve = sb("zve", [P, T])
        zrs = sb("zrs", [P, T])
        z_hat = sb("z_hat", [P, T, C])
        z_t = sb("z_t", [P, T, P])
        gel = sb("gel", [P, T, C])
        x1 = sb("x1", [P, T, C])
        x1_res = sb("x1_res", [P, T, C])
        gst = sb("gst", [P, B, 6])
        gmv = sb("gmv", [P, B, 2])
        dev = sb("dev", [P, B])
        spread = sb("spread", [P, B])
        gmean = sb("gmean", [P, B])
        gve = sb("gve", [P, B])
        grs = sb("grs", [P, B])
        gscale = sb("gscale", [P, B])
        gms = sb("gms", [P, B])
        gshift = sb("gshift", [P, B])
        x_gn = sb("x_gn", [P, B, HW])
        q1 = sb("q1", [P, B, HW])
        k1 = sb("k1", [P, B, HW])
        v1 = sb("v1", [P, B, S, C + 1])
        smax1 = sb("smax1", [P, T])
        nmax1 = sb("nmax1", [P, T])
        p1 = sb("p1", [P, 2, HW])
        p1_t = sb("p1_t", [P, 2, S, P])
        rec1 = sb("rec1", [P, T])
        y = sb("y", [P, T, C])

        names = """x_in0 x_in1 small_in large_in rows_in lnrow_in xst_in
            consts kblk_zero ones_set vones_set v1ones_set
            stats aggr sdev rstd_ok nmr_ok hat_ok xg_ok xln_ok
            fold1 fold1_out fold1_cols fold2 fold2_out fold3 fold3_out msab msab_out xres_ok
            q_bias q_mm q_out diag_a diag_p diag_v qh_mm qh_out
            acc_ok conv_mm conv_sum_ok gelu_ok coord tanh_ok dx_ok dy_ok fx_ok ay_ok hx_ok hy_ok bilin_ok
            interp samp k_mm k_out kblk_ok kblk_p v_mm v_out
            s_mm smax_ok ssub_ok pt_mm exp_ok av_mm rec_ok att_ok attt_mm attt_ok msa_mm z_ok
            zst_ok zmv_ok zve_ok zrs_ok zhat_ok zt_mm zt_ok mlp_mm gel_ok x1_ok x1res_ok x1t_mm
            gst_ok gmv_ok gm_mm gmean_ok dev_ok spread_ok gv_mm gve_ok grs_ok gscale_ok gms_ok gshift_ok
            xgn_ok qk_mm q1_ok k1_ok v1_mm v1_ok s1_mm smax1_ok nmax1_ok p1_ok p1t_mm p1t_ok av1_mm rec1_ok y_ok
            y_out""".split()
        s = {n: sem(n) for n in names}

        block = ctx.enter_context(nc.Block())

        x_hw_dram = x.rearrange("b (s p) c -> p b s c", p=P)
        x_st_dram = x.rearrange("b (p s) c -> p b (s c)", s=S)
        out_dram = out.rearrange("b (p s) c -> p b (s c)", s=S)

        taps = [(ky, kx) for ky in range(KS) for kx in range(KS)]
        centre = [(3, 3), (4, 4)]
        rest = [t for t in taps if t not in centre]
        N_PE = 24
        pe_taps = [centre[0]] + rest[:N_PE - 1]
        dve_taps = [centre[1]] + rest[N_PE - 1:]
        ACT_D = [i for i in range(N_PE) if i % 3 != 2]
        DVE_D = [i for i in range(N_PE) if i % 3 == 2]

        def tap_views(ky, kx, dst):
            ry, ay, y0, y1 = tap_range(ky, OH)
            rx, ax, x0, x1_ = tap_range(kx, OW)
            src = q_conv[:, :].rearrange("c (r yb t x) -> c r yb t x", r=2, t=2, x=OW)[
                :, ry, B * (y0 + ay):B * (y1 + ay), rx, x0 + ax:x1_ + ax]
            return src, dst.rearrange("c (yb x) -> c yb x", x=OW)[:, B * y0:B * y1, x0:x1_]

        def value_half(copy, eng, e):
            h = slice(e * PIX, (e + 1) * PIX)
            eng.wait_ge(s["v_mm"], 1)
            eng.wait_ge(s["vones_set"], 1)
            copy(v_blk[h, :, :, e * HD:(e + 1) * HD].rearrange("p b j d -> p (b j) d"),
                 bank[2][h, 0:B * PAIRS * HD].rearrange("p (n d) -> p n d", d=HD)).then_inc(s["v_out"], 1)

        @block.sync
        def _(sp):
            for h in range(2):
                sp.dma_start(x_hw[:, 4 * h:4 * h + 4, :].rearrange("p (b s) c -> p b s c", s=S),
                             x_hw_dram[:, 2 * h:2 * h + 2]).then_inc(s[f"x_in{h}"], 16)
            sp.dma_start(lg[:, :], large).then_inc(s["large_in"], 16)
            sp.dma_start(x_st[:, :, :], x_st_dram).then_inc(s["xst_in"], 16)
            for b in range(B):
                sp.wait_ge(s["y_ok"], 2 * b + 2)
                sp.dma_start(out_dram[:, b, :], y[:, 2 * b:2 * b + 2, :].rearrange("p s c -> p (s c)")).then_inc(s["y_out"], 16)
            sp.wait_ge(s["y_out"], 16 * B)

        @block.gpsimd
        def _(pool):
            pool.memset(ones_row[:, :], 1.0).then_inc(s["ones_set"], 1)
            pool.memset(eps[:, 0:1], LN_EPS)
            pool.memset(eps[:, 1:2], GN_EPS)
            pool.memset(neg_half[:, :], -0.5).then_inc(s["consts"], 1)
            pool.memset(v1[:, :, :, C:C + 1], 1.0).then_inc(s["v1ones_set"], 1)
            pool.memset(v_blk[:, :, :, 0:2 * HD], 0.0)
            pool.wait_ge(s["small_in"], 16)
            pool.tensor_copy(v_blk[:, :, :, 2 * HD:VW],
                             w("ones_mask").unsqueeze(1).unsqueeze(1).to_broadcast([P, B, PAIRS, 2])).then_inc(s["vones_set"], 1)
            pool.wait_ge(s["msab_out"], 1)
            pool.wait_ge(s["xst_in"], 16)
            pool.tensor_tensor(x_res[:, :, :], x_st[:, :, :].rearrange("p b (s c) -> p (b s) c", s=S),
                               msa_bias[:, :].unsqueeze(1).to_broadcast([P, T, C]), ALU.add).then_inc(s["xres_ok"], 1)
            for b in range(2, B):
                pool.wait_ge(s["k_out"], 1)
                pool.tensor_tensor(k_blk[:, b], k_t[:, b].unsqueeze(1).to_broadcast([P, NH, PIX]),
                                   w("head_of").unsqueeze(2).to_broadcast([P, NH, PIX]), ALU.mult).then_inc(s["kblk_p"], 1)
            for b in range(B):
                t0 = 2 * b
                pool.wait_ge(s["zve_ok"], b + 1)
                pool.tensor_tensor(zrs[:, t0:t0 + 2], zve[:, t0:t0 + 2], neg_half[:, 0:2], ALU.pow).then_inc(s["zrs_ok"], 1)
            for b in range(B):
                pool.wait_ge(s["x1_ok"], b + 1)
                pool.wait_ge(s["fold3_out"], 1)
                pool.tensor_tensor(x1_res[:, 2 * b:2 * b + 2, :], x1[:, 2 * b:2 * b + 2, :],
                                   out_bias[:, :].unsqueeze(1).to_broadcast([P, S, C]), ALU.add).then_inc(s["x1res_ok"], 1)
                pool.wait_ge(s["gve_ok"], b + 1)
                pool.tensor_tensor(grs[:, b:b + 1], gve[:, b:b + 1], neg_half[:, 0:1], ALU.pow).then_inc(s["grs_ok"], 1)

        @block.scalar
        def _(act):
            act.dma_start(sm[:, :], small).then_inc(s["small_in"], 16)
            act.dma_start(gb[:, :], ln_rows.partition_broadcast(P)).then_inc(s["lnrow_in"], 16)
            act.dma_start(row[:, :], rows).then_inc(s["rows_in"], 16)

            def build_diag(i):
                ky, kx = pe_taps[i]
                t = ky * KS + kx
                act.activation(diag[:, i, :], w("ident"), ACT.Copy, scale=w("dw_w")[:, t:t + 1]).then_inc(s["diag_a"], 1)

            act.wait_ge(s["small_in"], 16)
            act.wait_ge(s["consts"], 1)
            for h in range(2):
                act.wait_ge(s["aggr"], 4 * h + 4)
                act.activation(sd[:, 4 * h:4 * h + 4], mv[:, 4 * h:4 * h + 4, 1], ACT.Sqrt, bias=eps[:, 0:1]).then_inc(s["sdev"], 1)
            for i in range(T):
                if i % 4 == 0:
                    act.wait_ge(s["nmr_ok"], i // 4 + 1)
                act.activation(x_hat[:, i], x_hw[:, i], ACT.Identity, bias=nmr[:, i:i + 1],
                               scale=rstd[:, i:i + 1]).then_inc(s["hat_ok"], 1)
            for i in ACT_D:
                build_diag(i)
            act.wait_ge(s["fold1"], 1)
            act.copy(m_q[:, :], bank[6][:, 0:C]).then_inc(s["fold1_out"], 1)
            for j, name in enumerate(("mq_b", "mk_b", "mv_b")):
                act.activation(cols[:, j:j + 1], bank[6][:, C + j:C + j + 1], ACT.Identity,
                               bias=w(name)).then_inc(s["fold1_cols"], 1)
            act.wait_ge(s["fold2"], 1)
            act.copy(m_kv[:, :], bank[7][:, 0:2 * C]).then_inc(s["fold2_out"], 1)
            act.wait_ge(s["msab"], 1)
            act.copy(msa_bias[:, :], bank[7][:, 0:C]).then_inc(s["msab_out"], 1)
            act.wait_ge(s["fold3"], 1)
            act.copy(w_vo[:, :], bank[2][:, 0:C])
            act.copy(out_bias[:, :], bank[2][:, C:2 * C]).then_inc(s["fold3_out"], 1)
            qv = q_conv[:, :].rearrange("c (r y b t) -> c b r y t", r=2, y=OH, b=B)
            for b in range(2):
                act.wait_ge(s["q_mm"], 1)
                act.copy(qv[:, b], bank[0][:, b * HW:(b + 1) * HW].rearrange("c (r y t) -> c r y t", r=2, y=OH)).then_inc(s["q_out"], 1)
            act.wait_ge(s["fold1_cols"], 3)
            for g in range(2):
                act.wait_ge(s["qh_mm"], g + 1)
                act.activation(qh[:, g * 512:(g + 1) * 512], bank[4 + g][:, :], ACT.Identity, bias=cols[:, 0:1]).then_inc(s["qh_out"], 1)
            act.wait_ge(s["conv_sum_ok"], 1)
            act.activation(o_act[:, :, :, :].rearrange("c b y x -> c y b x"),
                           conv_sum[:, :].rearrange("c (y b x) -> c y b x", b=B, x=OW), ACT.Gelu, bias=w("dw_b")).then_inc(s["gelu_ok"], 1)
            act.wait_ge(s["coord"], 1)
            act.activation(tanh[:, :, :], bank[7][:, :].rearrange("p (d q) -> p d q", d=2), ACT.Tanh).then_inc(s["tanh_ok"], 1)
            act.wait_ge(s["dy_ok"], S)
            act.activation(abs_y[:, :], dist_y[:, :, :, :].rearrange("p s b q -> p (s b q)"), ACT.Abs).then_inc(s["ay_ok"], 1)
            act.wait_ge(s["ay_ok"], 1)
            act.activation(hat_y[:, :, :].rearrange("p s q -> p (s q)"), abs_y[:, :], ACT.Relu, scale=-1.0, bias=1.0).then_inc(s["hy_ok"], 1)
            act.wait_ge(s["interp"], 1)
            act.copy(sampled[:, :, :].rearrange("p b t -> p (b t)"), bank[0][:, 0:B * PIX]).then_inc(s["samp"], 1)
            act.wait_ge(s["k_mm"], 1)
            act.activation(k_t[:, :, :].rearrange("c b q -> c (b q)"), bank[1][:, 0:B * PIX], ACT.Identity, bias=cols[:, 1:2]).then_inc(s["k_out"], 1)
            value_half(act.copy, act, 1)

            def exp_tile(i):
                act.wait_ge(s["pt_mm"], i + 1)
                if i >= 2:
                    act.wait_ge(s["av_mm"], i - 1)
                act.activation(p_t[:, i % 2].rearrange("p j q -> p (j q)"), bank[5 + i % 2][:, :], ACT.Exp).then_inc(s["exp_ok"], 1)

            def att_tile(i):
                act.wait_ge(s["attt_mm"], i + 1)
                if i >= 2:
                    act.wait_ge(s["msa_mm"], i - 1)
                act.copy(att_t[:, i % 2], bank[0][:, 0:P]).then_inc(s["attt_ok"], 1)

            def zt_image(b):
                act.wait_ge(s["zt_mm"], b + 1)
                act.activation(z_t[:, 2 * b:2 * b + 2, :].rearrange("c s q -> c (s q)"), bank[2][:, 0:HW], ACT.Identity,
                               scale=w("ln_g"), bias=w("ln_b")).then_inc(s["zt_ok"], 1)

            for i in range(T + 4):
                if 2 <= i < T + 2:
                    att_tile(i - 2)
                if i < T:
                    exp_tile(i)
                if i >= 5 and i % 2 == 1:
                    zt_image((i - 5) // 2)
            for b in range(B):
                act.wait_ge(s["mlp_mm"], b + 1)
                act.activation(gel[:, 2 * b:2 * b + 2, :].rearrange("p s c -> p (s c)"), bank[3 + b][:, 0:HW], ACT.Gelu).then_inc(s["gel_ok"], 1)
            for b in range(B):
                act.wait_ge(s["gshift_ok"], b + 1)
                act.activation(x_gn[:, b], bank[b % 2][:, 0:HW], ACT.Identity, scale=gscale[:, b:b + 1],
                               bias=gshift[:, b:b + 1]).then_inc(s["xgn_ok"], 1)
                act.wait_ge(s["v1_mm"], b + 1)
                act.copy(v1[:, b, :, 0:C], bank[3][:, 0:HW].rearrange("p (s c) -> p s c", s=S)).then_inc(s["v1_ok"], 1)
                for t in range(S):
                    i = 2 * b + t
                    act.wait_ge(s["nmax1_ok"], b + 1)
                    if i >= 2:
                        act.wait_ge(s["p1t_mm"], i - 1)
                    act.activation(p1[:, i % 2], bank[4 + b % 2][:, t * HW:(t + 1) * HW], ACT.Exp, scale=C ** -0.5,
                                   bias=nmax1[:, i:i + 1]).then_inc(s["p1_ok"], 1)

        @block.vector
        def _(dve):
            for h in range(2):
                dve.wait_ge(s[f"x_in{h}"], 16)
                for i in range(4 * h, 4 * h + 4):
                    dve.bn_stats(st[:, i], x_hw[:, i]).then_inc(s["stats"], 1)
                for i in range(4 * h, 4 * h + 4):
                    dve.wait_ge(s["stats"], i + 1)
                    dve.bn_aggr(mv[:, i], st[:, i]).then_inc(s["aggr"], 1)
            for h in range(2):
                t = slice(4 * h, 4 * h + 4)
                dve.wait_ge(s["sdev"], h + 1)
                dve.reciprocal(rstd[:, t], sd[:, t]).then_inc(s["rstd_ok"], 1)
                dve.wait_ge(s["rstd_ok"], h + 1)
                dve.scalar_tensor_tensor(out=nmr[:, t], in0=mv[:, t, 0], scalar=-1.0, in1=rstd[:, t],
                                         op0=ALU.mult, op1=ALU.mult).then_inc(s["nmr_ok"], 1)
            dve.wait_ge(s["small_in"], 16)
            for n, i in enumerate(DVE_D[:4]):
                ky, kx = pe_taps[i]
                t = ky * KS + kx
                dve.tensor_scalar(diag[:, i, :], w("ident"), w("dw_w")[:, t:t + 1], None, ALU.mult).then_inc(s["diag_v"], 1)
            for h in range(2):
                t = slice(4 * h, 4 * h + 4)
                dve.wait_ge(s["hat_ok"], 4 * h + 4)
                dve.wait_ge(s["lnrow_in"], 16)
                dve.tensor_tensor(x_g[:, t], x_hat[:, t], gb[:, 0:C].unsqueeze(1).to_broadcast([P, 4, C]), ALU.mult).then_inc(s["xg_ok"], 1)
                dve.wait_ge(s["xg_ok"], h + 1)
                dve.tensor_tensor(x_ln[:, t], x_g[:, t], gb[:, C:2 * C].unsqueeze(1).to_broadcast([P, 4, C]), ALU.add).then_inc(s["xln_ok"], 1)
            for n, i in enumerate(DVE_D[4:]):
                ky, kx = pe_taps[i]
                t = ky * KS + kx
                dve.tensor_scalar(diag[:, i, :], w("ident"), w("dw_w")[:, t:t + 1], None, ALU.mult).then_inc(s["diag_v"], 1)
            qv = q_conv[:, :].rearrange("c (r y b t) -> c b r y t", r=2, y=OH, b=B)
            dve.wait_ge(s["q_mm"], 2)
            for b in range(2, B):
                dve.tensor_copy(qv[:, b], bank[1][:, (b - 2) * HW:(b - 1) * HW].rearrange("c (r y t) -> c r y t", r=2, y=OH)).then_inc(s["q_out"], 1)
            dve.wait_ge(s["q_out"], B)
            for n, (ky, kx) in enumerate(dve_taps):
                src, dst = tap_views(ky, kx, acc[:, :])
                wt = w("dw_w")[:, ky * KS + kx:ky * KS + kx + 1]
                if n == 0:
                    dve.tensor_scalar(dst, src, wt, None, ALU.mult).then_inc(s["acc_ok"], 1)
                else:
                    dve.wait_ge(s["acc_ok"], n)
                    dve.scalar_tensor_tensor(out=dst, in0=src, scalar=wt, in1=dst, op0=ALU.mult, op1=ALU.add).then_inc(s["acc_ok"], 1)
            dve.wait_ge(s["acc_ok"], len(dve_taps))
            dve.wait_ge(s["conv_mm"], 1)
            dve.tensor_tensor(conv_sum[:, :], bank[3][:, 0:B * PIX], acc[:, :], ALU.add).then_inc(s["conv_sum_ok"], 1)
            dve.wait_ge(s["tanh_ok"], 1)
            gx, gy = w("grid_x"), w("grid_y").rearrange("p (s q) -> p s q", s=S)
            scale = (H / R) / 2 * 0.5 * (W - 1)
            for t in range(S):
                dve.scalar_tensor_tensor(out=dist_y[:, t], in0=tanh[:, 1].rearrange("p (b q) -> p b q", b=B), scalar=scale,
                                         in1=gy[:, t].unsqueeze(1).to_broadcast([P, B, PIX]),
                                         op0=ALU.mult, op1=ALU.add).then_inc(s["dy_ok"], 1)
            dve.scalar_tensor_tensor(out=dist_x[:, :, :], in0=tanh[:, 0].rearrange("p (b q) -> p b q", b=B), scalar=scale,
                                     in1=gx.unsqueeze(1).to_broadcast([P, B, PIX]),
                                     op0=ALU.mult, op1=ALU.add).then_inc(s["dx_ok"], 1)
            dve.wait_ge(s["dx_ok"], 1)
            dve.tensor_scalar(falling_x[:, :], dist_x[:, :, :].rearrange("p b q -> p (b q)"), -1.0, 1.0, ALU.mult, ALU.add).then_inc(s["fx_ok"], 1)
            dve.wait_ge(s["fx_ok"], 1)
            dve.scalar_tensor_tensor(out=hat_x[:, :], in0=dist_x[:, :, :].rearrange("p b q -> p (b q)"), scalar=1.0,
                                     in1=falling_x[:, :], op0=ALU.add, op1=ALU.min).then_inc(s["hx_ok"], 1)
            dve.wait_ge(s["hx_ok"], 1)
            dve.wait_ge(s["hy_ok"], 1)
            dve.scalar_tensor_tensor(out=bilin[:, :, :, :].rearrange("p s b q -> p s (b q)"),
                                     in0=hat_x[:, :].unsqueeze(1).to_broadcast([P, S, B * PIX]), scalar=0.0,
                                     in1=hat_y[:, :, :], op0=ALU.max, op1=ALU.mult).then_inc(s["bilin_ok"], 1)
            dve.wait_ge(s["k_out"], 1)
            for b in range(2):
                dve.tensor_tensor(k_blk[:, b], k_t[:, b].unsqueeze(1).to_broadcast([P, NH, PIX]),
                                  w("head_of").unsqueeze(2).to_broadcast([P, NH, PIX]), ALU.mult).then_inc(s["kblk_ok"], 1)
            value_half(dve.tensor_copy, dve, 0)

            def shift_tile(i):
                sc = bank[3 + i % 2][:, :].rearrange("p (h q) -> p h q", h=NH)
                dve.wait_ge(s["s_mm"], i + 1)
                dve.tensor_reduce(smax[:, i % 2], sc, AX.X, ALU.max).then_inc(s["smax_ok"], 1)
                dve.wait_ge(s["smax_ok"], i + 1)
                if i >= 2:
                    dve.wait_ge(s["pt_mm"], i - 1)
                dve.tensor_tensor(s_sub[:, i % 2], sc, smax[:, i % 2].unsqueeze(2).to_broadcast([P, NH, PIX]),
                                  ALU.subtract).then_inc(s["ssub_ok"], 1)

            def norm_tile(i):
                av = bank[7][:, 0:PAIRS * VW].rearrange("p (j d) -> p j d", d=VW)
                dve.wait_ge(s["av_mm"], i + 1)
                dve.reciprocal(recip[:, i % 2].rearrange("p (j e) -> p j e", e=2), av[:, :, 2 * HD:VW]).then_inc(s["rec_ok"], 1)
                dve.wait_ge(s["rec_ok"], i + 1)
                if i >= 2:
                    dve.wait_ge(s["attt_mm"], i - 1)
                dve.tensor_tensor(att[:, i % 2].rearrange("p (j e d) -> p j e d", j=PAIRS, e=2),
                                  av[:, :, 0:2 * HD].rearrange("p j (e d) -> p j e d", e=2),
                                  recip[:, i % 2].rearrange("p (j e) -> p j e", e=2).unsqueeze(3).to_broadcast([P, PAIRS, 2, HD]),
                                  ALU.mult).then_inc(s["att_ok"], 1)

            def z_tile(i):
                dve.wait_ge(s["msa_mm"], i + 1)
                dve.wait_ge(s["xres_ok"], 1)
                dve.tensor_tensor(z[:, i], bank[1][:, 0:C], x_res[:, i], ALU.add).then_inc(s["z_ok"], 1)
                dve.wait_ge(s["z_ok"], i + 1)
                dve.bn_stats(zst[:, i], z[:, i]).then_inc(s["zst_ok"], 1)
                dve.wait_ge(s["zst_ok"], i + 1)
                dve.bn_aggr(zmv[:, i], zst[:, i]).then_inc(s["zmv_ok"], 1)
                if i % 2 == 1:
                    dve.wait_ge(s["zmv_ok"], i + 1)
                    dve.tensor_scalar(zve[:, i - 1:i + 1], zmv[:, i - 1:i + 1, 1], LN_EPS, None, ALU.add).then_inc(s["zve_ok"], 1)

            def zhat_image(b):
                dve.wait_ge(s["zrs_ok"], b + 1)
                for i in (2 * b, 2 * b + 1):
                    dve.tensor_scalar(z_hat[:, i], z[:, i], zmv[:, i, 0:1], zrs[:, i:i + 1], ALU.subtract, ALU.mult).then_inc(s["zhat_ok"], 1)

            shift_tile(0)
            for i in range(T + 3):
                if i + 1 < T:
                    shift_tile(i + 1)
                if 2 <= i < T + 2:
                    z_tile(i - 2)
                if 1 <= i < T + 1:
                    norm_tile(i - 1)
                if i >= 4 and i % 2 == 0:
                    zhat_image((i - 4) // 2)
            for b in range(B):
                t0 = 2 * b
                dve.wait_ge(s["gel_ok"], b + 1)
                dve.tensor_tensor(x1[:, t0:t0 + 2], gel[:, t0:t0 + 2], z[:, t0:t0 + 2], ALU.add).then_inc(s["x1_ok"], 1)

            def gn_image(b):
                bi = slice(b, b + 1)
                dve.wait_ge(s["x1t_mm"], b + 1)
                dve.bn_stats(gst[:, b], bank[b % 2][:, 0:HW]).then_inc(s["gst_ok"], 1)
                dve.wait_ge(s["gst_ok"], b + 1)
                dve.bn_aggr(gmv[:, b], gst[:, b]).then_inc(s["gmv_ok"], 1)
                dve.wait_ge(s["gm_mm"], b + 1)
                dve.tensor_copy(gmean[:, bi], bank[3][:, 0:1]).then_inc(s["gmean_ok"], 1)
                dve.wait_ge(s["gmean_ok"], b + 1)
                dve.tensor_scalar(dev[:, bi], gmv[:, b, 0:1], gmean[:, bi], None, ALU.subtract).then_inc(s["dev_ok"], 1)
                dve.wait_ge(s["dev_ok"], b + 1)
                dve.scalar_tensor_tensor(out=spread[:, bi], in0=dev[:, bi], scalar=dev[:, bi], in1=gmv[:, b, 1:2],
                                         op0=ALU.mult, op1=ALU.add).then_inc(s["spread_ok"], 1)
                dve.wait_ge(s["gv_mm"], b + 1)
                dve.tensor_scalar(gve[:, bi], bank[3][:, 1:2], GN_EPS, None, ALU.add).then_inc(s["gve_ok"], 1)
                dve.wait_ge(s["grs_ok"], b + 1)
                dve.tensor_scalar(gscale[:, bi], grs[:, bi], w("gn_gamma"), None, ALU.mult).then_inc(s["gscale_ok"], 1)
                dve.wait_ge(s["gscale_ok"], b + 1)
                dve.tensor_scalar(gms[:, bi], gmean[:, bi], gscale[:, bi], None, ALU.mult).then_inc(s["gms_ok"], 1)
                dve.wait_ge(s["gms_ok"], b + 1)
                dve.tensor_scalar(gshift[:, bi], gms[:, bi], -1.0, w("gn_beta"), ALU.mult, ALU.add).then_inc(s["gshift_ok"], 1)

            def attend_image(b):
                dve.wait_ge(s["qk_mm"], b + 1)
                dve.tensor_scalar(q1[:, b], bank[2][:, 0:HW], w("bq1"), None, ALU.add).then_inc(s["q1_ok"], 1)
                dve.tensor_scalar(k1[:, b], bank[2][:, HW:2 * HW], w("bk1"), None, ALU.add).then_inc(s["k1_ok"], 1)
                dve.wait_ge(s["s1_mm"], b + 1)
                t = slice(2 * b, 2 * b + 2)
                dve.tensor_reduce(smax1[:, t], bank[4 + b % 2][:, :].rearrange("p (t m) -> p t m", t=2), AX.X, ALU.max).then_inc(s["smax1_ok"], 1)
                dve.wait_ge(s["smax1_ok"], b + 1)
                dve.tensor_scalar(nmax1[:, t], smax1[:, t], -C ** -0.5, None, ALU.mult).then_inc(s["nmax1_ok"], 1)

            def finish_image(b):
                for t in range(S):
                    i = 2 * b + t
                    dve.wait_ge(s["p1t_mm"], i + 1)
                    if i >= 2:
                        dve.wait_ge(s["av1_mm"], (i - 2) + 1)
                    dve.tensor_copy(p1_t[:, i % 2].rearrange("p s q -> p (s q)"), bank[6][:, 0:HW]).then_inc(s["p1t_ok"], 1)
                    dve.wait_ge(s["av1_mm"], i + 1)
                    dve.reciprocal(rec1[:, i:i + 1], bank[7][:, C:C + 1]).then_inc(s["rec1_ok"], 1)
                    dve.wait_ge(s["rec1_ok"], i + 1)
                    dve.wait_ge(s["x1res_ok"], b + 1)
                    dve.scalar_tensor_tensor(out=y[:, i], in0=bank[7][:, 0:C], scalar=rec1[:, i:i + 1], in1=x1_res[:, i],
                                             op0=ALU.mult, op1=ALU.add).then_inc(s["y_ok"], 1)

            gn_image(0)
            for b in range(B):
                if b + 1 < B:
                    gn_image(b + 1)
                attend_image(b)
                finish_image(b)

        @block.tensor
        def _(pe):
            def mm(o, l, r_, start=True, stop=True, **k):
                return pe.matmul(o, l, r_, start=start, stop=stop, **k)

            pe.wait_ge(s["small_in"], 16)
            pe.wait_ge(s["large_in"], 16)
            pe.wait_ge(s["rows_in"], 16)
            pe.wait_ge(s["ones_set"], 1)
            mm(bank[6][:, 0:C], w("wqT"), w("mq_w"))
            mm(bank[6][:, C:C + 1], w("mq_w"), w("bq"))
            mm(bank[6][:, C + 1:C + 2], w("mk_w"), w("bv"))
            mm(bank[6][:, C + 2:C + 3], w("mv_w"), w("bv")).then_inc(s["fold1"], 1)
            a0 = LARGE_AT["mk_w"][0]
            mm(bank[7][:, 0:2 * C], w("wvT"), lg[:, a0:a0 + 2 * C]).then_inc(s["fold2"], 1)
            mm(bank[2][:, 0:C], w("wv1T"), w("wo1"))
            mm(bank[2][:, C:2 * C], w("bv1").to_broadcast([P, P]), w("wo1"), stop=False)
            mm(bank[2][:, C:2 * C], ones_row[:, :], r("bo1"), start=False).then_inc(s["fold3"], 1)
            for g in range(2):
                for b in range(2):
                    mm(bank[g][:, b * HW:(b + 1) * HW], ones_row[:, :],
                       r("bq_conv").rearrange("o (r n) -> o r n", r=2).unsqueeze(2).to_broadcast([1, 2, S, C // 2]),
                       start=(b == 0), stop=False, skip_group_check=True)
            for i in range(T):
                b, t = divmod(i, S)
                if i % 4 == 0:
                    pe.wait_ge(s["xln_ok"], i // 4 + 1)
                o = bank[b // 2][:, (b % 2) * HW:(b % 2 + 1) * HW].rearrange("c (r s n) -> c r s n", r=2, s=S)[:, :, t]
                m = mm(o, x_ln[:, i], w("wq_conv"), start=False, skip_group_check=True)
                if i % 4 == 3:
                    m.then_inc(s["q_mm"], 1)
            pe.wait_ge(s["fold1_cols"], 3)
            pe.wait_ge(s["fold2_out"], 1)
            mm(bank[7][:, 0:C], cols[:, 2:3].to_broadcast([P, P]), w("mo_w"), stop=False)
            mm(bank[7][:, 0:C], ones_row[:, :], r("mo_b"), start=False).then_inc(s["msab"], 1)
            pe.wait_ge(s["q_out"], B)
            for n, (ky, kx) in enumerate(pe_taps):
                if n in ACT_D:
                    pe.wait_ge(s["diag_a"], ACT_D.index(n) + 1)
                else:
                    pe.wait_ge(s["diag_v"], DVE_D.index(n) + 1)
                src, dst = tap_views(ky, kx, bank[3][:, 0:B * PIX])
                m = mm(dst, diag[:, n, :], src, start=(n == 0), stop=(n == N_PE - 1), skip_group_check=True)
            m.then_inc(s["conv_mm"], 1)
            pe.wait_ge(s["fold1_out"], 1)
            for g in range(2):
                mm(bank[4 + g][:, :], m_q[:, :], x_ln[:, 4 * g:4 * g + 4, :].rearrange("p t c -> p (t c)")).then_inc(s["qh_mm"], 1)
            pe.wait_ge(s["gelu_ok"], 1)
            pe.wait_ge(s["msab_out"], 1)
            for d in range(2):
                m = mm(bank[7][:, d * 256:(d + 1) * 256], w("pw")[:, 1 - d:2 - d].to_broadcast([P, P]),
                       o_act[:, :, :, :].rearrange("c b y x -> c (b y x)"))
            m.then_inc(s["coord"], 1)
            pe.wait_ge(s["bilin_ok"], 1)
            for b in range(B):
                for t in range(S):
                    for e in range(2):
                        m = mm(bank[0][e * PIX:(e + 1) * PIX, b * PIX:(b + 1) * PIX], bilin[:, t, b],
                               x_hw[:, 2 * b + t].rearrange("p (t e) -> p t e", e=2)[:, :, e],
                               start=(t == 0), stop=(t == S - 1))
            m.then_inc(s["interp"], 1)
            pe.wait_ge(s["samp"], 1)
            mm(bank[1][:, 0:B * PIX], m_kv[:, 0:C], sampled[:, :, :].rearrange("p b t -> p (b t)")).then_inc(s["k_mm"], 1)
            pe.wait_ge(s["fold3_out"], 1)
            for b in range(B):
                for e in range(2):
                    m = mm(bank[2][e * PIX:(e + 1) * PIX, b * PIX:(b + 1) * PIX], sampled[:, b],
                           m_kv[:, C:2 * C].rearrange("p (j e d) -> p j e d", j=PAIRS, e=2)[:, :, e])
            m.then_inc(s["v_mm"], 1)

            def score_tile(i):
                b = i // S
                if b < 2:
                    pe.wait_ge(s["kblk_ok"], b + 1)
                else:
                    pe.wait_ge(s["kblk_p"], b - 1)
                if i == 0:
                    pe.wait_ge(s["conv_sum_ok"], 1)
                if i % 4 == 0:
                    pe.wait_ge(s["qh_out"], i // 4 + 1)
                if i == 1:
                    pe.wait_ge(s["qh_out"], 2)
                if i >= 2:
                    pe.wait_ge(s["ssub_ok"], i - 1)
                mm(bank[3 + i % 2][:, :], qh[:, i * P:(i + 1) * P], k_blk[:, b].rearrange("p h q -> p (h q)")).then_inc(s["s_mm"], 1)

            def transpose_scores(i):
                pe.wait_ge(s["ssub_ok"], i + 1)
                if i >= 2:
                    pe.wait_ge(s["exp_ok"], i - 1)
                for j in range(PAIRS):
                    m = pe.transpose(bank[5 + i % 2][:, j * P:(j + 1) * P],
                                     s_sub[:, i % 2, 2 * j:2 * j + 2].rearrange("p h q -> p (h q)"), w("ident"))
                m.then_inc(s["pt_mm"], 1)

            def value_tile(i):
                b = i // S
                pe.wait_ge(s["exp_ok"], i + 1)
                if i == 0:
                    pe.wait_ge(s["v_out"], 2)
                if i >= 1:
                    pe.wait_ge(s["att_ok"], i)
                for j in range(PAIRS):
                    m = mm(bank[7][:, j * VW:(j + 1) * VW], p_t[:, i % 2, j], v_blk[:, b, j])
                m.then_inc(s["av_mm"], 1)

            def att_transpose(i):
                pe.wait_ge(s["att_ok"], i + 1)
                if i >= 1:
                    pe.wait_ge(s["attt_ok"], i)
                pe.transpose(bank[0][:, 0:P], att[:, i % 2], w("ident")).then_inc(s["attt_mm"], 1)

            def out_project(i):
                pe.wait_ge(s["attt_ok"], i + 1)
                if i == 0:
                    pe.wait_ge(s["k_out"], 1)
                if i >= 1:
                    pe.wait_ge(s["z_ok"], i)
                mm(bank[1][:, 0:C], att_t[:, i % 2], w("mo_w")).then_inc(s["msa_mm"], 1)

            def z_transpose(b):
                pe.wait_ge(s["zhat_ok"], 2 * b + 2)
                if b >= 1:
                    pe.wait_ge(s["zt_ok"], b)
                for t in range(S):
                    m = pe.transpose(bank[2][:, t * P:(t + 1) * P], z_hat[:, 2 * b + t], w("ident"))
                m.then_inc(s["zt_mm"], 1)

            score_tile(0)
            for i in range(T + 4):
                if i >= 5 and i % 2 == 1:
                    z_transpose((i - 5) // 2)
                if 2 <= i < T + 2:
                    att_transpose(i - 2)
                if i + 1 < T:
                    score_tile(i + 1)
                if 2 <= i < T + 2:
                    out_project(i - 2)
                if i < T:
                    transpose_scores(i)
                if 1 <= i < T + 1:
                    value_tile(i - 1)

            for b in range(B):
                pe.wait_ge(s["zt_ok"], b + 1)
                for t in range(S):
                    i = 2 * b + t
                    o = bank[3 + b][:, t * C:(t + 1) * C]
                    mm(o, z_t[:, i], w("mlp_w"), stop=False)
                    m = mm(o, ones_row[:, :], r("mlp_b"), start=False)
                m.then_inc(s["mlp_mm"], 1)

            def x1_transpose(b):
                pe.wait_ge(s["x1_ok"], b + 1)
                if b >= 2:
                    pe.wait_ge(s["xgn_ok"], b - 1)
                for t in range(S):
                    m = pe.transpose(bank[b % 2][:, t * P:(t + 1) * P], x1[:, 2 * b + t], w("ident"))
                m.then_inc(s["x1t_mm"], 1)

            def gn_image(b):
                pe.wait_ge(s["gmv_ok"], b + 1)
                if b == 0:
                    pe.wait_ge(s["gel_ok"], 1)
                if b >= 1:
                    pe.wait_ge(s["v1_ok"], b)
                mm(bank[3][:, 0:1], w("group_mean"), gmv[:, b, 0:1]).then_inc(s["gm_mm"], 1)
                pe.wait_ge(s["spread_ok"], b + 1)
                mm(bank[3][:, 1:2], w("group_mean"), spread[:, b:b + 1]).then_inc(s["gv_mm"], 1)

            def project(b):
                pe.wait_ge(s["xgn_ok"], b + 1)
                if b >= 1:
                    pe.wait_ge(s["k1_ok"], b)
                mm(bank[2][:, 0:HW], w("wq1"), x_gn[:, b])
                mm(bank[2][:, HW:2 * HW], w("wk1"), x_gn[:, b]).then_inc(s["qk_mm"], 1)
                pe.wait_ge(s["gve_ok"], b + 1)
                for t in range(S):
                    m = mm(bank[3][:, t * C:(t + 1) * C], x_gn[:, b, t * P:(t + 1) * P], w_vo[:, :])
                m.then_inc(s["v1_mm"], 1)

            def score_image(b):
                pe.wait_ge(s["q1_ok"], b + 1)
                pe.wait_ge(s["k1_ok"], b + 1)
                if b < 2:
                    pe.wait_ge(s["gel_ok"], b + 2)
                else:
                    pe.wait_ge(s["p1_ok"], 2 * (b - 1))
                for t in range(S):
                    m = mm(bank[4 + b % 2][:, t * HW:(t + 1) * HW], q1[:, b, t * P:(t + 1) * P], k1[:, b])
                m.then_inc(s["s1_mm"], 1)

            def value_image(b):
                for t in range(S):
                    i = 2 * b + t
                    pe.wait_ge(s["p1_ok"], i + 1)
                    if i == 0:
                        pe.wait_ge(s["gel_ok"], B)
                    if i >= 1:
                        pe.wait_ge(s["p1t_ok"], i)
                    for j in range(S):
                        m = pe.transpose(bank[6][:, j * P:(j + 1) * P], p1[:, i % 2, j * P:(j + 1) * P], w("ident"))
                    m.then_inc(s["p1t_mm"], 1)
                    pe.wait_ge(s["p1t_ok"], i + 1)
                    pe.wait_ge(s["v1_ok"], b + 1)
                    pe.wait_ge(s["v1ones_set"], 1)
                    if i >= 1:
                        pe.wait_ge(s["y_ok"], i)
                    for j in range(S):
                        m = mm(bank[7][:, 0:C + 1], p1_t[:, i % 2, j], v1[:, b, j], start=(j == 0), stop=(j == S - 1))
                    m.then_inc(s["av1_mm"], 1)

            x1_transpose(0)
            x1_transpose(1)
            gn_image(0)
            project(0)
            for b in range(B):
                if b + 2 < B:
                    x1_transpose(b + 2)
                if b + 1 < B:
                    gn_image(b + 1)
                score_image(b)
                value_image(b)
                if b + 1 < B:
                    project(b + 1)


def kernel(**inputs):
    import numpy as np
    import concourse.bacc as bacc
    from concourse.bass_utils import run_bass_kernel_spmd as run

    get = {k: np.asarray(v) for k, v in inputs.items()}
    L0, L1 = "L0_conv_", "L1_conv_"
    p = np.arange(P)
    f32 = np.float32

    const = {
        "ident": np.eye(P, dtype=f32),
        "head_of": (p[:, None] // HD == np.arange(NH)[None, :]).astype(f32),
        "ones_mask": (p[:, None] // PIX == np.arange(2)[None, :]).astype(f32),
        "group_mean": ((p[:, None] // GROUP == p[None, :] // GROUP) / GROUP).astype(f32),
    }
    half = np.arange(OH) + 0.5
    centre = ((half * (2.0 / OH)) * (H / R) / 2.0 + 1.0) * 0.5 * (W - 1)
    const["grid_x"] = (np.tile(centre, OH)[None, :] - (p % W)[:, None]).astype(f32)
    const["grid_y"] = np.concatenate(
        [np.repeat(centre, OW)[None, :] - (t * (P // W) + p // W)[:, None] for t in range(S)], axis=1).astype(f32)

    col = lambda a: a.reshape(C, 1)
    conv_order = lambda a: a.reshape(-1, OH // 2, 2, OW, 2).transpose(0, 2, 1, 4, 3).reshape(-1, C)
    data = {
        "dw_w": get[L0 + "dw_w"].reshape(C, KS * KS), "pw": get[L0 + "pw_w"].reshape(2, C).T,
        "wq_conv": conv_order(get[L0 + "wq"]), "wqT": get[L0 + "wq"].T, "wvT": get[L0 + "wv"].T,
        "wv1T": get[L1 + "wv"].T, "wo1": get[L1 + "wo"], "wq1": get[L1 + "wq"], "wk1": get[L1 + "wk"],
        "bq1": col(get[L1 + "bq"]), "bk1": col(get[L1 + "bk"]), "bv1": col(get[L1 + "bv"]),
        "gn_gamma": col(get[L1 + "gn_gamma"]), "gn_beta": col(get[L1 + "gn_beta"]),
    }
    for n in ("dw_b", "bq", "mq_b", "bv", "mk_b", "mv_b", "ln_g", "ln_b"):
        data[n] = col(get[L0 + n])
    for n in ("mq_w", "mk_w", "mv_w", "mo_w", "mlp_w"):
        data[n] = get[L0 + n]
    row = {"bq_conv": conv_order(get[L0 + "bq"].reshape(1, C)), "mo_b": get[L0 + "mo_b"].reshape(1, C),
           "mlp_b": get[L0 + "mlp_b"].reshape(1, C), "bo1": get[L1 + "bo"].reshape(1, C)}

    arrays = {
        "x": np.ascontiguousarray(get["x"]).reshape(B, HW, C),
        "small": np.ascontiguousarray(np.concatenate([const[n] if n in const else data[n] for n, _ in SMALL], axis=1)),
        "large": np.ascontiguousarray(np.concatenate([data[n] for n, _ in LARGE], axis=1)),
        "rows": np.ascontiguousarray(np.concatenate([row[n] for n in ROWS], axis=1)),
        "ln_rows": np.ascontiguousarray(np.concatenate([get[L0 + "ln_g"], get[L0 + "ln_b"]])),
    }
    nc = bacc.Bacc("TRN2", target_bir_lowering=False, num_devices=1)
    args = [nc.dram_tensor(n, a.shape, mybir.dt.from_np(a.dtype), kind="ExternalInput").ap() for n, a in arrays.items()]
    out = nc.dram_tensor("out", (B, HW, C), F32, kind="ExternalOutput").ap()
    build(nc, *args, out)
    got = run(nc, [arrays], core_ids=[0]).results[0]["out"]
    return got.reshape(B, H, W, C)
```

```python
from contextlib import ExitStack

import concourse.bass as bass
from concourse import mybir
from concourse.alu_op_type import AluOpType as ALU

F32 = mybir.dt.float32
BF16 = mybir.dt.bfloat16
ACT = mybir.ActivationFunctionType
AX = mybir.AxisListType

P = 128
B, H, W, C = 4, 16, 16, 128
HW = H * W
S = HW // P
T = B * S
NH = 8
HD = C // NH
G = 2
PAIRS = NH // 2
KS, R = 7, 2
OH, OW = H // R, W // R
PIX = OH * OW
VW = 2 * HD + 2
LN_EPS, GN_EPS = 1e-5, 1e-6
GROUP = C // 32
N_PE, N_POOL = 16, 13
N_DIAG_DVE, N_DIAG_POOL = 3, 2
N_WARM = 10

PACKS = {
    "early": [("dw_w", KS * KS), ("ln_g", 1), ("ln_b", 1), ("pw", 2), ("dw_b", 1), ("bq", 1), ("mq_b", 1), ("bv", 1),
              ("mk_b", 1), ("mv_b", 1), ("gn_gamma", 1), ("gn_beta", 1), ("bq1", 1), ("bk1", 1), ("bv1", 1),
              ("ident", P), ("wq_conv", C)],
    "fold": [("wqT", C), ("mq_w", C), ("wvT", C), ("mk_w", C), ("mv_w", C)],
    "mid": [("mo_w", C), ("head_of", NH), ("ones_mask", 2), ("grid_x", G * PIX), ("grid_y", S * G * PIX)],
    "late": [("mlp_w", C), ("wv1T", C), ("wo1", C), ("wq1", C), ("wk1", C), ("group_mean", P)],
}
ROWS = ["bq_conv", "ln_b", "mo_b", "mlp_b", "bo1"]


def columns(parts):
    at, out = 0, {}
    for name, n in parts:
        out[name] = (at, at + n)
        at += n
    return out, at


PLACE = {pack: columns(parts) for pack, parts in PACKS.items()}


def tap_range(k, n):
    shift, phase = divmod(k - KS // 2, R)
    return phase, shift, max(0, -shift), min(n, n - shift)


def reach(tap):
    n = 1
    for k, size in zip(tap, (OH, OW)):
        _, _, a, b = tap_range(k, size)
        n *= b - a
    return n


def share_taps():
    first = {"pe": (3, 3), "dve0": (4, 4), "dve1": (3, 4), "pool": (4, 3)}
    taps = [(ky, kx) for ky in range(KS) for kx in range(KS)]
    rest = sorted((t for t in taps if t not in first.values()), key=reach)
    pool, rest = rest[:N_POOL - 1], rest[N_POOL - 1:]
    pe, dve = rest[:N_PE - 1], rest[N_PE - 1:]
    return [first["pe"]] + pe, [first["dve0"], first["dve1"]] + dve, [first["pool"]] + pool


PE_TAPS, DVE_TAPS, POOL_TAPS = share_taps()


def build(nc, x, early, fold, mid, late, rows, ln_rows, out):
    ctx = ExitStack()
    with ctx:
        def sb(name, shape, dt=F32):
            return ctx.enter_context(nc.sbuf_tensor(name, shape, dt))

        def sem(name):
            return ctx.enter_context(nc.semaphore(name))

        bank = [ctx.enter_context(nc.psum_tensor(f"bank{i}", [P, 512], F32)) for i in range(8)]

        x_hw = sb("x_hw", [P, T, C])
        x_st = sb("x_st", [P, B, S * C])
        packs = {n: sb(f"pack_{n}", [P, PLACE[n][1]]) for n in PACKS}
        row = sb("row", [1, len(ROWS) * C])
        gb = sb("gb", [P, 2 * C])
        ones_row = sb("ones_row", [1, P])
        ones_col = sb("ones_col", [P, 1])
        warm = sb("warm", [P, 512], BF16)
        eps = sb("eps", [P, 1])
        neg_half = sb("neg_half", [P, B])

        def w(name):
            for n, (at, _) in PLACE.items():
                if name in at:
                    return packs[n][:, at[name][0]:at[name][1]]
            raise KeyError(name)

        def r(name):
            i = ROWS.index(name)
            return row[:, i * C:(i + 1) * C]

        st = sb("st", [P, T, 6])
        mv = sb("mv", [P, T, 2])
        sd = sb("sd", [P, T])
        rstd = sb("rstd", [P, T])
        x_hat = sb("x_hat", [P, T, C])
        x_g = sb("x_g", [P, T, C])
        x_ln = sb("x_ln", [P, T, C])
        colsum = sb("colsum", [1, C])
        q_bias = sb("q_bias", [P, HW])
        m_q = sb("m_q", [P, C])
        m_kv = sb("m_kv", [P, 2 * C])
        w_vo = sb("w_vo", [P, C])
        cols = sb("cols", [P, 3])
        cols1 = sb("cols1", [P, 2])
        wq1g = sb("wq1g", [P, C])
        wk1g = sb("wk1g", [P, C])
        w_vog = sb("w_vog", [P, C])
        mlp_wg = sb("mlp_wg", [P, C])
        mlp_row = sb("mlp_row", [1, C])
        msa_bias = sb("msa_bias", [P, C])
        out_bias = sb("out_bias", [P, C])
        x_res = sb("x_res", [P, T, C])
        diag = sb("diag", [P, len(PE_TAPS), P])
        q_conv = sb("q_conv", [P, 2 * OH * B * 2 * OW])
        acc = sb("acc", [P, 3, OH * B * OW])
        prod = sb("prod", [P, len(POOL_TAPS), OH * B * OW])
        o_act = sb("o_act", [P, B, OH, OW])
        qh = sb("qh", [P, T * P])
        tanh = sb("tanh", [P, 2, 2, G * PIX])
        dist_x = sb("dist_x", [P, 2, G * PIX])
        dist_y = sb("dist_y", [P, 2, S, G * PIX])
        falling_x = sb("falling_x", [P, 2, G * PIX])
        abs_y = sb("abs_y", [P, 2, S * G * PIX])
        hat_x = sb("hat_x", [P, 2, G * PIX])
        hat_y = sb("hat_y", [P, 2, S, G * PIX])
        bilin = sb("bilin", [P, 2, S, G * PIX])
        sampled = sb("sampled", [P, B, PIX])
        k_t = sb("k_t", [P, B, PIX])
        k_blk = sb("k_blk", [P, B, NH, PIX])
        v_blk = sb("v_blk", [P, B, PAIRS, VW])
        smax = sb("smax", [P, 2, NH])
        s_sub = sb("s_sub", [P, 2, NH, PIX])
        p_t = sb("p_t", [P, 2, PAIRS, P])
        recip = sb("recip", [P, 2, NH])
        att = sb("att", [P, 2, C])
        att_t = sb("att_t", [P, 2, P])
        z = sb("z", [P, T, C])
        zst = sb("zst", [P, T, 6])
        zmv = sb("zmv", [P, T, 2])
        zve = sb("zve", [P, T])
        zrs = sb("zrs", [P, T])
        z_hat = sb("z_hat", [P, T, C])
        z_t = sb("z_t", [P, T, P])
        gel = sb("gel", [P, T, C])
        x1 = sb("x1", [P, T, C])
        x1_res = sb("x1_res", [P, T, C])
        gst = sb("gst", [P, B, 6])
        gmv = sb("gmv", [P, B, 2])
        gmean = sb("gmean", [P, B])
        dev = sb("dev", [P, B])
        dev2 = sb("dev2", [P, B])
        spread = sb("spread", [P, B])
        gve = sb("gve", [P, B])
        grs = sb("grs", [P, B])
        gnm = sb("gnm", [P, B])
        x_gn = sb("x_gn", [P, B, HW])
        q1 = sb("q1", [P, B, HW])
        k1 = sb("k1", [P, B, HW])
        v1 = sb("v1", [P, B, S, C + 1])
        smax1 = sb("smax1", [P, T])
        nmax1 = sb("nmax1", [P, T])
        p1 = sb("p1", [P, 2, S, HW])
        p1_t = sb("p1_t", [P, 2, S, S, P])
        rec1 = sb("rec1", [P, T])
        y = sb("y", [P, T, C])

        names = """x_in0 x_in1 early_in fold_in mid_in late_in rows_in lnrow_in xst_in
            ones_set consts vones_set v1ones_set warm_set
            stats aggr sdev rstd_ok hat_ok xg_ok xln_ok
            colsum_mm colsum_ok qbias_mm qbias_ok
            fold1 fold1_out fold1_cols fold2 fold2_out fold3 fold3_out out_bias_mm out_bias_ok msab msab_out
            mlp_wg_ok cols1_ok mlp_row_ok gamma_ok xres_ok
            q_mm q_out diag_a diag_v diag_p qh_mm qh_out
            acc0_ok acc1_ok prod_ok accp_ok conv_mm gelu_ok coord tanh_ok dx_ok dy_ok fx_ok ay_ok hx_ok hy_ok bilin_ok
            interp samp k_mm k_out kblk_ok kblk_p v_mm v_even v_odd
            s_mm smax_ok ssub_ok pt_mm exp_ok av_mm rec_ok att_ok attt_mm attt_ok msa_mm z_ok
            zst_ok zmv_ok zve_ok zrs_ok zhat_ok zt_mm zt_ok mlp_mm gel_ok x1_ok x1res_ok x1t_mm
            gst_ok gmv_ok gm_mm gmean_ok dev_ok dev2_ok spread_ok gv_mm gve_ok grs_ok gnm_ok
            xgn_v xgn_a qk_mm q1_ok k1_ok v1_mm v1_ok s1_mm smax1_ok nmax1_ok p1_ok p1t_mm p1t_ok av1_mm rec1_ok y_ok
            y_out""".split()
        s = {n: sem(n) for n in names}

        block = ctx.enter_context(nc.Block())

        x_hw_dram = x.rearrange("b (s p) c -> p b s c", p=P)
        x_st_dram = x.rearrange("b (p s) c -> p b (s c)", s=S)
        out_dram = out.rearrange("b (p s) c -> p b (s c)", s=S)

        def halves(h):
            return slice(4 * h, 4 * h + 4)

        def tap_views(tap, dst):
            ry, ay, y0, y1 = tap_range(tap[0], OH)
            rx, ax, x0, x1_ = tap_range(tap[1], OW)
            src = q_conv[:, :].rearrange("c (r yb t x) -> c r yb t x", r=2, t=2, x=OW)[
                :, ry, B * (y0 + ay):B * (y1 + ay), rx, x0 + ax:x1_ + ax]
            return src, dst.rearrange("c (yb x) -> c yb x", x=OW)[:, B * y0:B * y1, x0:x1_]

        def tap_weight(tap):
            i = tap[0] * KS + tap[1]
            return w("dw_w")[:, i:i + 1]

        DVE_D = list(range(0, N_DIAG_DVE))
        POOL_D = list(range(len(PE_TAPS) - N_DIAG_POOL, len(PE_TAPS)))
        ACT_D = [i for i in range(len(PE_TAPS)) if i not in DVE_D + POOL_D]

        GN_SETS = [range(0, 3), range(3, 4)]

        def value_half(copy, eng, e, g, done):
            h = slice(e * PIX, (e + 1) * PIX)
            eng.wait_ge(s["v_mm"], g + 1)
            eng.wait_ge(s["vones_set"], 1)
            copy(v_blk[h, 2 * g:2 * g + 2, :, e * HD:(e + 1) * HD].rearrange("p b j d -> p (b j) d"),
                 bank[g][h, 0:G * PAIRS * HD].rearrange("p (n d) -> p n d", d=HD)).then_inc(done, 1)

        def wait_xgn(eng, b):
            eng.wait_ge(s["xgn_v"] if b % 2 == 0 else s["xgn_a"], b // 2 + 1)

        @block.sync
        def _(sp):
            for h in range(2):
                if h == 1:
                    sp.dma_start(packs["early"][:, :], early).then_inc(s["early_in"], 16)
                    sp.dma_start(row[:, :], rows).then_inc(s["rows_in"], 16)
                sp.dma_start(x_hw[:, halves(h), :].rearrange("p (b s) c -> p b s c", s=S),
                             x_hw_dram[:, 2 * h:2 * h + 2]).then_inc(s[f"x_in{h}"], 16)
            sp.dma_start(packs["fold"][:, :], fold).then_inc(s["fold_in"], 16)
            sp.dma_start(gb[:, :], ln_rows.partition_broadcast(P)).then_inc(s["lnrow_in"], 16)
            sp.dma_start(packs["mid"][:, :], mid).then_inc(s["mid_in"], 16)
            sp.dma_start(x_st[:, :, :], x_st_dram).then_inc(s["xst_in"], 16)
            sp.dma_start(packs["late"][:, :], late).then_inc(s["late_in"], 16)
            for b in range(B):
                sp.wait_ge(s["y_ok"], 2 * b + 2)
                sp.dma_start(out_dram[:, b, :], y[:, 2 * b:2 * b + 2, :].rearrange("p s c -> p (s c)")).then_inc(s["y_out"], 16)
            sp.wait_ge(s["y_out"], 16 * B)

        @block.gpsimd
        def _(pool):
            pool.memset(warm[:, :], 0.0).then_inc(s["warm_set"], 1)
            pool.memset(ones_row[:, :], 1.0)
            pool.memset(ones_col[:, :], 1.0).then_inc(s["ones_set"], 1)
            pool.memset(eps[:, :], LN_EPS)
            pool.memset(neg_half[:, :], -0.5).then_inc(s["consts"], 1)
            pool.memset(v1[:, :, :, C:C + 1], 1.0).then_inc(s["v1ones_set"], 1)
            pool.memset(v_blk[:, :, :, 0:2 * HD], 0.0)
            pool.wait_ge(s["early_in"], 16)
            for i in POOL_D:
                pool.tensor_scalar(diag[:, i, :], w("ident"), tap_weight(PE_TAPS[i]), None, ALU.mult).then_inc(s["diag_p"], 1)

            def norm_affine(h):
                t = halves(h)
                pool.wait_ge(s["hat_ok"], 4 * h + 4)
                pool.wait_ge(s["lnrow_in"], 16)
                pool.tensor_tensor(x_g[:, t], x_hat[:, t], gb[:, 0:C].unsqueeze(1).to_broadcast([P, 4, C]), ALU.mult).then_inc(s["xg_ok"], 1)
                pool.wait_ge(s["xg_ok"], h + 1)
                pool.tensor_tensor(x_ln[:, t], x_g[:, t], gb[:, C:2 * C].unsqueeze(1).to_broadcast([P, 4, C]), ALU.add).then_inc(s["xln_ok"], 1)

            norm_affine(0)
            for n, tap in enumerate(POOL_TAPS):
                if n == 0:
                    continue
                _, dst = tap_views(tap, acc[:, 2, :])
                _, src = tap_views(tap, prod[:, n, :])
                pool.wait_ge(s["prod_ok"], n + 1)
                if n >= 2:
                    pool.wait_ge(s["accp_ok"], n - 1)
                pool.tensor_tensor(dst, dst, src, ALU.add).then_inc(s["accp_ok"], 1)
            norm_affine(1)
            pool.wait_ge(s["mid_in"], 16)
            pool.tensor_copy(v_blk[:, :, :, 2 * HD:VW],
                             w("ones_mask").unsqueeze(1).unsqueeze(1).to_broadcast([P, B, PAIRS, 2])).then_inc(s["vones_set"], 1)
            pool.wait_ge(s["msab_out"], 1)
            pool.wait_ge(s["xst_in"], 16)
            pool.tensor_tensor(x_res[:, :, :], x_st[:, :, :].rearrange("p b (s c) -> p (b s) c", s=S),
                               msa_bias[:, :].unsqueeze(1).to_broadcast([P, T, C]), ALU.add).then_inc(s["xres_ok"], 1)
            for b in range(G, B):
                pool.wait_ge(s["k_out"], 2)
                pool.tensor_tensor(k_blk[:, b], k_t[:, b].unsqueeze(1).to_broadcast([P, NH, PIX]),
                                   w("head_of").unsqueeze(2).to_broadcast([P, NH, PIX]), ALU.mult).then_inc(s["kblk_p"], 1)
            pool.wait_ge(s["late_in"], 16)
            pool.tensor_scalar(mlp_wg[:, :], w("mlp_w"), w("ln_g"), None, ALU.mult).then_inc(s["mlp_wg_ok"], 1)
            for b in range(B):
                pool.wait_ge(s["zve_ok"], b + 1)
                pool.tensor_tensor(zrs[:, 2 * b:2 * b + 2], zve[:, 2 * b:2 * b + 2], neg_half[:, 0:2], ALU.pow).then_inc(s["zrs_ok"], 1)
                if b == 0:
                    pool.tensor_scalar(wq1g[:, :], w("wq1"), w("gn_gamma"), None, ALU.mult)
                    pool.tensor_scalar(wk1g[:, :], w("wk1"), w("gn_gamma"), None, ALU.mult)
                    pool.wait_ge(s["fold3_out"], 1)
                    pool.tensor_scalar(w_vog[:, :], w_vo[:, :], w("gn_gamma"), None, ALU.mult).then_inc(s["gamma_ok"], 1)

            def residual(b):
                pool.wait_ge(s["x1_ok"], b + 1)
                pool.wait_ge(s["out_bias_ok"], 1)
                pool.tensor_tensor(x1_res[:, 2 * b:2 * b + 2, :], x1[:, 2 * b:2 * b + 2, :],
                                   out_bias[:, :].unsqueeze(1).to_broadcast([P, S, C]), ALU.add).then_inc(s["x1res_ok"], 1)

            for n, images in enumerate(GN_SETS):
                a, b = images.start, images.stop
                pool.wait_ge(s["gve_ok"], n + 1)
                pool.tensor_tensor(grs[:, a:b], gve[:, a:b], neg_half[:, a:b], ALU.pow).then_inc(s["grs_ok"], 1)
                for b in images:
                    residual(b)

        @block.scalar
        def _(act):
            act.wait_ge(s["consts"], 1)
            act.wait_ge(s["early_in"], 16)
            for i in ACT_D[:4]:
                act.activation(diag[:, i, :], w("ident"), ACT.Copy, scale=tap_weight(PE_TAPS[i])).then_inc(s["diag_a"], 1)
            for h in range(2):
                act.wait_ge(s["aggr"], 4 * h + 4)
                act.activation(sd[:, halves(h)], mv[:, halves(h), 1], ACT.Sqrt, bias=eps[:, 0:1]).then_inc(s["sdev"], 1)
                for i in ACT_D[4 + 4 * h:8 + 4 * h]:
                    act.activation(diag[:, i, :], w("ident"), ACT.Copy, scale=tap_weight(PE_TAPS[i])).then_inc(s["diag_a"], 1)
            for i in ACT_D[12:]:
                act.activation(diag[:, i, :], w("ident"), ACT.Copy, scale=tap_weight(PE_TAPS[i])).then_inc(s["diag_a"], 1)
            act.wait_ge(s["colsum_mm"], 1)
            act.copy(colsum[:, :], bank[5][0:1, 0:C]).then_inc(s["colsum_ok"], 1)
            act.wait_ge(s["qbias_mm"], 1)
            act.copy(q_bias[:, :], bank[5][:, 0:HW]).then_inc(s["qbias_ok"], 1)
            act.wait_ge(s["q_out"], 2 * B)
            for n, tap in enumerate(POOL_TAPS):
                src, dst = tap_views(tap, acc[:, 2, :] if n == 0 else prod[:, n, :])
                act.activation(dst, src, ACT.Copy, scale=tap_weight(tap)).then_inc(s["prod_ok"], 1)
            act.wait_ge(s["fold1"], 1)
            act.copy(m_q[:, :], bank[6][:, 0:C]).then_inc(s["fold1_out"], 1)
            for j, name in enumerate(("mq_b", "mk_b", "mv_b")):
                act.activation(cols[:, j:j + 1], bank[6][:, C + j:C + j + 1], ACT.Identity,
                               bias=w(name)).then_inc(s["fold1_cols"], 1)
            act.wait_ge(s["fold2"], 1)
            act.copy(m_kv[:, :], bank[7][:, 0:2 * C]).then_inc(s["fold2_out"], 1)
            act.wait_ge(s["conv_mm"], 1)
            act.activation(o_act[:, :, :, :].rearrange("c b y x -> c y b x"),
                           bank[3][:, 0:B * PIX].rearrange("c (y b x) -> c y b x", b=B, x=OW), ACT.Gelu, bias=w("dw_b")).then_inc(s["gelu_ok"], 1)
            for g in range(2):
                act.wait_ge(s["coord"], g + 1)
                act.activation(tanh[:, g].rearrange("p d q -> p (d q)"), bank[7 - g][:, 0:2 * G * PIX], ACT.Tanh).then_inc(s["tanh_ok"], 1)
            act.wait_ge(s["fold1_cols"], 3)
            act.wait_ge(s["qh_mm"], 1)
            act.activation(qh[:, 0:512], bank[4][:, :], ACT.Identity, bias=cols[:, 0:1]).then_inc(s["qh_out"], 1)
            for g in range(2):
                act.wait_ge(s["dy_ok"], g + 1)
                act.activation(abs_y[:, g], dist_y[:, g].rearrange("p s q -> p (s q)"), ACT.Abs).then_inc(s["ay_ok"], 1)
                act.wait_ge(s["ay_ok"], g + 1)
                act.activation(hat_y[:, g].rearrange("p s q -> p (s q)"), abs_y[:, g], ACT.Relu, scale=-1.0, bias=1.0).then_inc(s["hy_ok"], 1)
            act.wait_ge(s["msab"], 1)
            act.copy(msa_bias[:, :], bank[2][:, 0:C]).then_inc(s["msab_out"], 1)

            def sample_half(g):
                act.wait_ge(s["interp"], g + 1)
                act.copy(sampled[:, 2 * g:2 * g + 2, :].rearrange("p b t -> p (b t)"), bank[g][:, 0:G * PIX]).then_inc(s["samp"], 1)

            def key_half(g):
                act.wait_ge(s["k_mm"], g + 1)
                act.activation(k_t[:, 2 * g:2 * g + 2, :].rearrange("c b q -> c (b q)"), bank[2][:, 0:G * PIX], ACT.Identity,
                               bias=cols[:, 1:2]).then_inc(s["k_out"], 1)

            sample_half(0)
            key_half(0)
            value_half(act.copy, act, 1, 0, s["v_odd"])
            sample_half(1)
            act.wait_ge(s["qh_mm"], 2)
            act.activation(qh[:, 512:1024], bank[5][:, :], ACT.Identity, bias=cols[:, 0:1]).then_inc(s["qh_out"], 1)
            key_half(1)
            value_half(act.copy, act, 1, 1, s["v_odd"])

            def exp_tile(i):
                act.wait_ge(s["pt_mm"], i + 1)
                if i >= 2:
                    act.wait_ge(s["av_mm"], i - 1)
                act.activation(p_t[:, i % 2].rearrange("p j q -> p (j q)"), bank[5 + i % 2][:, :], ACT.Exp).then_inc(s["exp_ok"], 1)

            def att_tile(i):
                act.wait_ge(s["attt_mm"], i + 1)
                if i >= 2:
                    act.wait_ge(s["msa_mm"], i - 1)
                act.copy(att_t[:, i % 2], bank[0][:, 0:P]).then_inc(s["attt_ok"], 1)

            def zt_image(b):
                act.wait_ge(s["zt_mm"], b + 1)
                act.copy(z_t[:, 2 * b:2 * b + 2, :].rearrange("c s q -> c (s q)"), bank[2][:, 0:HW]).then_inc(s["zt_ok"], 1)

            for i in range(T + 1):
                if 2 <= i:
                    att_tile(i - 2)
                if i < T:
                    exp_tile(i)
                if i == 1:
                    act.wait_ge(s["fold3"], 1)
                    act.copy(mlp_row[:, :], bank[2][0:1, C:2 * C]).then_inc(s["mlp_row_ok"], 1)
                    act.copy(w_vo[:, :], bank[2][:, 0:C]).then_inc(s["fold3_out"], 1)
                    for j, name in enumerate(("bq1", "bk1")):
                        act.activation(cols1[:, j:j + 1], bank[2][:, 2 * C + j:2 * C + j + 1], ACT.Identity, bias=w(name)).then_inc(s["cols1_ok"], 1)
                if i == 2:
                    act.wait_ge(s["out_bias_mm"], 1)
                    act.copy(out_bias[:, :], bank[2][:, 0:C]).then_inc(s["out_bias_ok"], 1)
                if i >= 6 and i % 2 == 0:
                    zt_image((i - 6) // 2)
            def gelu_image(b):
                act.wait_ge(s["mlp_mm"], b + 1)
                act.activation(gel[:, 2 * b:2 * b + 2, :].rearrange("p s c -> p (s c)"), bank[3 + b][:, 0:HW], ACT.Gelu).then_inc(s["gel_ok"], 1)

            gelu_image(0)
            att_tile(T - 1)
            gelu_image(1)
            zt_image(2)
            gelu_image(2)

            def norm_image(b):
                n = 0 if b < 3 else 1
                act.wait_ge(s["gnm_ok"], n + 1)
                act.activation(x_gn[:, b], bank[3 + b][:, 0:HW], ACT.Identity, scale=grs[:, b:b + 1],
                               bias=gnm[:, b:b + 1]).then_inc(s["xgn_a"], 1)

            def value_copy(b):
                act.wait_ge(s["v1_mm"], b + 1)
                act.copy(v1[:, b, :, 0:C], bank[7][:, 0:HW].rearrange("p (s c) -> p s c", s=S)).then_inc(s["v1_ok"], 1)

            def exp_image(b):
                act.wait_ge(s["nmax1_ok"], b + 1)
                if b >= 2:
                    act.wait_ge(s["p1t_mm"], b - 1)
                for t in range(S):
                    act.activation(p1[:, b % 2, t], bank[3 + b % 2][:, t * HW:(t + 1) * HW], ACT.Exp, scale=C ** -0.5,
                                   bias=nmax1[:, 2 * b + t:2 * b + t + 1]).then_inc(s["p1_ok"], 1)

            def probs_image(b):
                act.wait_ge(s["p1t_mm"], b + 1)
                if b >= 2:
                    act.wait_ge(s["av1_mm"], 2 * (b - 1))
                act.copy(p1_t[:, b % 2].rearrange("p t j q -> p (t j q)"), bank[5][:, :]).then_inc(s["p1t_ok"], 1)

            zt_image(3)
            norm_image(1)
            value_copy(0)
            gelu_image(3)
            exp_image(0)
            value_copy(1)
            probs_image(0)
            norm_image(3)
            exp_image(1)
            value_copy(2)
            probs_image(1)
            exp_image(2)
            value_copy(3)
            probs_image(2)
            exp_image(3)
            probs_image(3)

        @block.vector
        def _(dve):
            for h in range(2):
                if h == 1:
                    dve.wait_ge(s["early_in"], 16)
                    for i in DVE_D:
                        dve.tensor_scalar(diag[:, i, :], w("ident"), tap_weight(PE_TAPS[i]), None, ALU.mult).then_inc(s["diag_v"], 1)
                dve.wait_ge(s[f"x_in{h}"], 16)
                for i in range(4 * h, 4 * h + 4):
                    dve.bn_stats(st[:, i], x_hw[:, i]).then_inc(s["stats"], 1)
                for i in range(4 * h, 4 * h + 4):
                    dve.wait_ge(s["stats"], i + 1)
                    dve.bn_aggr(mv[:, i], st[:, i]).then_inc(s["aggr"], 1)
            for h in range(2):
                dve.wait_ge(s["sdev"], h + 1)
                dve.reciprocal(rstd[:, halves(h)], sd[:, halves(h)]).then_inc(s["rstd_ok"], 1)
                dve.wait_ge(s["rstd_ok"], h + 1)
                for i in range(4 * h, 4 * h + 4):
                    dve.tensor_scalar(x_hat[:, i], x_hw[:, i], mv[:, i, 0:1], rstd[:, i:i + 1], ALU.subtract, ALU.mult).then_inc(s["hat_ok"], 1)
            qv = q_conv[:, :].rearrange("c (r y b t) -> c r y b t", r=2, y=OH, b=B)
            dve.wait_ge(s["qbias_ok"], 1)
            for b in range(B):
                if b % 2 == 0:
                    dve.wait_ge(s["q_mm"], b // 2 + 1)
                for ph in range(2):
                    at = (b % 2) * HW + ph * P
                    dve.scalar_tensor_tensor(
                        out=qv[:, ph, :, b], in0=bank[b // 2][:, at:at + P].rearrange("c (y t) -> c y t", y=OH), scalar=w("ln_g"),
                        in1=q_bias[:, ph * P:(ph + 1) * P].rearrange("c (y t) -> c y t", y=OH),
                        op0=ALU.mult, op1=ALU.add).then_inc(s["q_out"], 1)
            dve.wait_ge(s["q_out"], 2 * B)
            for n, tap in enumerate(DVE_TAPS):
                chain, k = n % 2, n // 2
                src, dst = tap_views(tap, acc[:, chain, :])
                if k == 0:
                    ins = dve.tensor_scalar(dst, src, tap_weight(tap), None, ALU.mult)
                else:
                    dve.wait_ge(s[f"acc{chain}_ok"], k)
                    ins = dve.scalar_tensor_tensor(out=dst, in0=src, scalar=tap_weight(tap), in1=dst, op0=ALU.mult, op1=ALU.add)
                ins.then_inc(s[f"acc{chain}_ok"], 1)
            gx, gy = w("grid_x"), w("grid_y").rearrange("p (s q) -> p s q", s=S)
            scale = (H / R) / 2 * 0.5 * (W - 1)

            def sample_weights(g):
                dve.wait_ge(s["tanh_ok"], g + 1)
                dve.wait_ge(s["mid_in"], 16)
                dve.scalar_tensor_tensor(out=dist_y[:, g], in0=tanh[:, g, 1].unsqueeze(1).to_broadcast([P, S, G * PIX]), scalar=scale,
                                         in1=gy, op0=ALU.mult, op1=ALU.add).then_inc(s["dy_ok"], 1)
                dve.scalar_tensor_tensor(out=dist_x[:, g], in0=tanh[:, g, 0], scalar=scale,
                                         in1=gx, op0=ALU.mult, op1=ALU.add).then_inc(s["dx_ok"], 1)
                dve.wait_ge(s["dx_ok"], g + 1)
                dve.tensor_scalar(falling_x[:, g], dist_x[:, g], -1.0, 1.0, ALU.mult, ALU.add).then_inc(s["fx_ok"], 1)
                dve.wait_ge(s["fx_ok"], g + 1)
                dve.scalar_tensor_tensor(out=hat_x[:, g], in0=dist_x[:, g], scalar=1.0,
                                         in1=falling_x[:, g], op0=ALU.add, op1=ALU.min).then_inc(s["hx_ok"], 1)

            def bilinear(g):
                dve.wait_ge(s["hx_ok"], g + 1)
                dve.wait_ge(s["hy_ok"], g + 1)
                dve.scalar_tensor_tensor(out=bilin[:, g], in0=hat_x[:, g].unsqueeze(1).to_broadcast([P, S, G * PIX]), scalar=0.0,
                                         in1=hat_y[:, g], op0=ALU.max, op1=ALU.mult).then_inc(s["bilin_ok"], 1)

            sample_weights(0)
            sample_weights(1)
            bilinear(0)
            bilinear(1)
            dve.wait_ge(s["k_out"], 1)
            for b in range(G):
                dve.tensor_tensor(k_blk[:, b], k_t[:, b].unsqueeze(1).to_broadcast([P, NH, PIX]),
                                  w("head_of").unsqueeze(2).to_broadcast([P, NH, PIX]), ALU.mult).then_inc(s["kblk_ok"], 1)
                if b == 0:
                    value_half(dve.tensor_copy, dve, 0, 0, s["v_even"])

            def scores(i):
                return bank[3 + i % 2][:, :].rearrange("p (h q) -> p h q", h=NH)

            def max_tile(i):
                dve.wait_ge(s["s_mm"], i + 1)
                dve.tensor_reduce(smax[:, i % 2], scores(i), AX.X, ALU.max).then_inc(s["smax_ok"], 1)

            def shift_tile(i):
                dve.wait_ge(s["smax_ok"], i + 1)
                if i >= 2:
                    dve.wait_ge(s["pt_mm"], i - 1)
                dve.tensor_tensor(s_sub[:, i % 2], scores(i), smax[:, i % 2].unsqueeze(2).to_broadcast([P, NH, PIX]),
                                  ALU.subtract).then_inc(s["ssub_ok"], 1)

            av = bank[7][:, 0:PAIRS * VW].rearrange("p (j d) -> p j d", d=VW)

            def recip_tile(i):
                dve.wait_ge(s["av_mm"], i + 1)
                dve.reciprocal(recip[:, i % 2].rearrange("p (j e) -> p j e", e=2), av[:, :, 2 * HD:VW]).then_inc(s["rec_ok"], 1)

            def norm_tile(i):
                dve.wait_ge(s["rec_ok"], i + 1)
                if i >= 2:
                    dve.wait_ge(s["attt_mm"], i - 1)
                dve.tensor_tensor(att[:, i % 2].rearrange("p (j e d) -> p j e d", j=PAIRS, e=2),
                                  av[:, :, 0:2 * HD].rearrange("p j (e d) -> p j e d", e=2),
                                  recip[:, i % 2].rearrange("p (j e) -> p j e", e=2).unsqueeze(3).to_broadcast([P, PAIRS, 2, HD]),
                                  ALU.mult).then_inc(s["att_ok"], 1)

            def z_tile(i):
                dve.wait_ge(s["msa_mm"], i + 1)
                dve.wait_ge(s["xres_ok"], 1)
                dve.tensor_tensor(z[:, i], bank[1][:, 0:C], x_res[:, i], ALU.add).then_inc(s["z_ok"], 1)

            def z_stats(i):
                dve.wait_ge(s["z_ok"], i + 1)
                dve.bn_stats(zst[:, i], z[:, i]).then_inc(s["zst_ok"], 1)

            def z_aggr(i):
                dve.wait_ge(s["zst_ok"], i + 1)
                dve.bn_aggr(zmv[:, i], zst[:, i]).then_inc(s["zmv_ok"], 1)

            def z_var(b):
                dve.wait_ge(s["zmv_ok"], 2 * b + 2)
                dve.tensor_scalar(zve[:, 2 * b:2 * b + 2], zmv[:, 2 * b:2 * b + 2, 1], LN_EPS, None, ALU.add).then_inc(s["zve_ok"], 1)

            def zhat_image(b):
                dve.wait_ge(s["zrs_ok"], b + 1)
                for i in (2 * b, 2 * b + 1):
                    dve.tensor_scalar(z_hat[:, i], z[:, i], zmv[:, i, 0:1], zrs[:, i:i + 1], ALU.subtract, ALU.mult).then_inc(s["zhat_ok"], 1)

            def x1_image(b):
                dve.wait_ge(s["gel_ok"], b + 1)
                dve.tensor_tensor(x1[:, 2 * b:2 * b + 2], gel[:, 2 * b:2 * b + 2], z[:, 2 * b:2 * b + 2], ALU.add).then_inc(s["x1_ok"], 1)

            max_tile(0)
            shift_tile(0)
            for i in range(T + 1):
                if i + 1 < T:
                    max_tile(i + 1)
                if i >= 3:
                    z_stats(i - 3)
                if i + 1 < T:
                    shift_tile(i + 1)
                if i >= 3:
                    z_aggr(i - 3)
                if i == 0:
                    value_half(dve.tensor_copy, dve, 0, 1, s["v_even"])
                if i >= 1:
                    recip_tile(i - 1)
                if i >= 2:
                    z_tile(i - 2)
                if i >= 1:
                    norm_tile(i - 1)
                if i >= 4 and i % 2 == 0:
                    z_var((i - 4) // 2)
                if i >= 5 and i % 2 == 1:
                    zhat_image((i - 5) // 2)

            def gn_stats(b):
                dve.wait_ge(s["x1t_mm"], b + 1)
                dve.bn_stats(gst[:, b], bank[3 + b][:, 0:HW]).then_inc(s["gst_ok"], 1)

            def gn_aggr(b):
                dve.wait_ge(s["gst_ok"], b + 1)
                dve.bn_aggr(gmv[:, b], gst[:, b]).then_inc(s["gmv_ok"], 1)

            def gn_set(n):
                i = slice(GN_SETS[n].start, GN_SETS[n].stop)
                k = i.stop - i.start
                dve.wait_ge(s["gm_mm"], n + 1)
                dve.tensor_copy(gmean[:, i], bank[7][:, 0:k]).then_inc(s["gmean_ok"], 1)
                dve.wait_ge(s["gmean_ok"], n + 1)
                dve.tensor_tensor(dev[:, i], gmv[:, i, 0], gmean[:, i], ALU.subtract).then_inc(s["dev_ok"], 1)
                dve.wait_ge(s["dev_ok"], n + 1)
                dve.tensor_tensor(dev2[:, i], dev[:, i], dev[:, i], ALU.mult).then_inc(s["dev2_ok"], 1)
                dve.wait_ge(s["dev2_ok"], n + 1)
                dve.tensor_tensor(spread[:, i], dev2[:, i], gmv[:, i, 1], ALU.add).then_inc(s["spread_ok"], 1)
                dve.wait_ge(s["gv_mm"], n + 1)
                dve.tensor_scalar(gve[:, i], bank[7][:, B:B + k], GN_EPS, None, ALU.add).then_inc(s["gve_ok"], 1)

            def gn_scale(n):
                i = slice(GN_SETS[n].start, GN_SETS[n].stop)
                dve.wait_ge(s["grs_ok"], n + 1)
                dve.scalar_tensor_tensor(out=gnm[:, i], in0=gmean[:, i], scalar=-1.0, in1=grs[:, i],
                                         op0=ALU.mult, op1=ALU.mult).then_inc(s["gnm_ok"], 1)

            def norm_image(b):
                dve.tensor_scalar(x_gn[:, b], bank[3 + b][:, 0:HW], gmean[:, b:b + 1], grs[:, b:b + 1],
                                  ALU.subtract, ALU.mult).then_inc(s["xgn_v"], 1)

            def project_out(b):
                dve.wait_ge(s["qk_mm"], b + 1)
                dve.wait_ge(s["cols1_ok"], 2)
                dve.tensor_scalar(q1[:, b], bank[b % 2][:, 0:HW], cols1[:, 0:1], None, ALU.add).then_inc(s["q1_ok"], 1)
                dve.tensor_scalar(k1[:, b], bank[b % 2][:, HW:2 * HW], cols1[:, 1:2], None, ALU.add).then_inc(s["k1_ok"], 1)

            def max_image(b):
                t = slice(2 * b, 2 * b + 2)
                dve.wait_ge(s["s1_mm"], b + 1)
                dve.tensor_reduce(smax1[:, t], bank[3 + b % 2][:, :].rearrange("p (t m) -> p t m", t=2), AX.X, ALU.max).then_inc(s["smax1_ok"], 1)
                dve.wait_ge(s["smax1_ok"], b + 1)
                dve.tensor_scalar(nmax1[:, t], smax1[:, t], -C ** -0.5, None, ALU.mult).then_inc(s["nmax1_ok"], 1)

            def finish_image(b):
                dve.wait_ge(s["x1res_ok"], b + 1)
                for t in range(S):
                    i = 2 * b + t
                    o = t * HW
                    dve.wait_ge(s["av1_mm"], 2 * b + 2)
                    dve.reciprocal(rec1[:, i:i + 1], bank[2][:, o + C:o + C + 1]).then_inc(s["rec1_ok"], 1)
                for t in range(S):
                    i = 2 * b + t
                    o = t * HW
                    dve.wait_ge(s["rec1_ok"], i + 1)
                    dve.scalar_tensor_tensor(out=y[:, i], in0=bank[2][:, o:o + C], scalar=rec1[:, i:i + 1], in1=x1_res[:, i],
                                             op0=ALU.mult, op1=ALU.add).then_inc(s["y_ok"], 1)

            z_tile(T - 1)
            z_stats(T - 2)
            z_aggr(T - 2)
            zhat_image(2)
            z_stats(T - 1)
            z_aggr(T - 1)
            z_var(3)
            x1_image(0)
            x1_image(1)
            zhat_image(3)
            x1_image(2)
            for b in range(3):
                gn_stats(b)
            for b in range(3):
                gn_aggr(b)
            gn_set(0)
            gn_scale(0)
            norm_image(0)
            norm_image(2)
            project_out(0)
            x1_image(3)
            project_out(1)
            gn_stats(3)
            gn_aggr(3)
            gn_set(1)
            max_image(0)
            gn_scale(1)
            project_out(2)
            max_image(1)
            finish_image(0)
            project_out(3)
            max_image(2)
            finish_image(1)
            max_image(3)
            finish_image(2)
            finish_image(3)

        @block.tensor
        def _(pe):
            def mm(o, l, r_, start=True, stop=True, **k):
                return pe.matmul(o, l, r_, start=start, stop=stop, **k)

            pe.wait_ge(s["warm_set"], 1)
            for _ in range(N_WARM):
                mm(bank[4][:, :], warm[:, 0:P], warm[:, :])
            pe.wait_ge(s["ones_set"], 1)
            pe.wait_ge(s["early_in"], 16)
            mm(bank[5][0:1, 0:C], ones_col[:, :], w("wq_conv")).then_inc(s["colsum_mm"], 1)

            def phases(a):
                return a.rearrange("o (r n) -> o r n", r=2).unsqueeze(2).to_broadcast([1, 2, S, C // 2])

            pe.wait_ge(s["colsum_ok"], 1)
            pe.wait_ge(s["rows_in"], 16)
            mm(bank[5][:, 0:HW], r("ln_b"), phases(colsum[:, :]), stop=False)
            mm(bank[5][:, 0:HW], ones_row[:, :], phases(r("bq_conv")), start=False).then_inc(s["qbias_mm"], 1)
            for i in range(T):
                b, t = divmod(i, S)
                pe.wait_ge(s["hat_ok"], i + 1)
                o = bank[b // 2][:, (b % 2) * HW:(b % 2 + 1) * HW].rearrange("c (r s n) -> c r s n", r=2, s=S)[:, :, t]
                m = mm(o, x_hat[:, i], w("wq_conv"))
                if i % 4 == 3:
                    m.then_inc(s["q_mm"], 1)
            pe.wait_ge(s["fold_in"], 16)
            mm(bank[6][:, 0:C], w("wqT"), w("mq_w"))
            mm(bank[6][:, C:C + 1], w("mq_w"), w("bq"))
            mm(bank[6][:, C + 1:C + 2], w("mk_w"), w("bv"))
            mm(bank[6][:, C + 2:C + 3], w("mv_w"), w("bv")).then_inc(s["fold1"], 1)
            a0 = PLACE["fold"][0]["mk_w"][0]
            mm(bank[7][:, 0:2 * C], w("wvT"), packs["fold"][:, a0:a0 + 2 * C]).then_inc(s["fold2"], 1)
            pe.wait_ge(s["q_out"], 2 * B)
            for n, tap in enumerate(PE_TAPS):
                for which, done in ((ACT_D, "diag_a"), (DVE_D, "diag_v"), (POOL_D, "diag_p")):
                    if n in which:
                        pe.wait_ge(s[done], which.index(n) + 1)
                src, dst = tap_views(tap, bank[3][:, 0:B * PIX])
                mm(dst, diag[:, n, :], src, start=(n == 0), stop=False, skip_group_check=True)
            for k, done, n in ((2, "accp_ok", len(POOL_TAPS) - 1), (1, "acc1_ok", len(DVE_TAPS) // 2),
                               (0, "acc0_ok", (len(DVE_TAPS) + 1) // 2)):
                pe.wait_ge(s[done], n)
                m = mm(bank[3][:, 0:B * PIX], w("ident"), acc[:, k, :], start=False, stop=(k == 0), skip_group_check=True)
            m.then_inc(s["conv_mm"], 1)

            def query_half(h):
                pe.wait_ge(s["fold1_out"], 1)
                pe.wait_ge(s["xln_ok"], h + 1)
                mm(bank[4 + h][:, :], m_q[:, :], x_ln[:, halves(h), :].rearrange("p t c -> p (t c)")).then_inc(s["qh_mm"], 1)

            query_half(0)
            pe.wait_ge(s["gelu_ok"], 1)
            pe.wait_ge(s["fold2_out"], 1)
            for g in range(2):
                for d in range(2):
                    m = mm(bank[7 - g][:, d * G * PIX:(d + 1) * G * PIX], w("pw")[:, 1 - d:2 - d].to_broadcast([P, P]),
                           o_act[:, 2 * g:2 * g + 2].rearrange("c b y x -> c (b y x)"))
                m.then_inc(s["coord"], 1)
            pe.wait_ge(s["fold1_cols"], 3)
            pe.wait_ge(s["mid_in"], 16)
            mm(bank[2][:, 0:C], cols[:, 2:3].to_broadcast([P, P]), w("mo_w"), stop=False)
            mm(bank[2][:, 0:C], ones_row[:, :], r("mo_b"), start=False).then_inc(s["msab"], 1)
            query_half(1)

            def sample_half(g):
                pe.wait_ge(s["bilin_ok"], g + 1)
                for b in range(G):
                    for t in range(S):
                        for e in range(2):
                            m = mm(bank[g][e * PIX:(e + 1) * PIX, b * PIX:(b + 1) * PIX], bilin[:, g, t, b * PIX:(b + 1) * PIX],
                                   x_hw[:, 2 * (G * g + b) + t].rearrange("p (t e) -> p t e", e=2)[:, :, e],
                                   start=(t == 0), stop=(t == S - 1))
                m.then_inc(s["interp"], 1)

            def key_half(g):
                pe.wait_ge(s["samp"], g + 1)
                if g == 0:
                    pe.wait_ge(s["msab_out"], 1)
                else:
                    pe.wait_ge(s["k_out"], 1)
                mm(bank[2][:, 0:G * PIX], m_kv[:, 0:C], sampled[:, 2 * g:2 * g + 2, :].rearrange("p b t -> p (b t)")).then_inc(s["k_mm"], 1)
                for b in range(G):
                    for e in range(2):
                        m = mm(bank[g][e * PIX:(e + 1) * PIX, b * PIX:(b + 1) * PIX], sampled[:, G * g + b],
                               m_kv[:, C:2 * C].rearrange("p (j e d) -> p j e d", j=PAIRS, e=2)[:, :, e])
                m.then_inc(s["v_mm"], 1)

            sample_half(0)
            key_half(0)
            sample_half(1)

            def score_tile(i):
                b = i // S
                if b < G:
                    pe.wait_ge(s["kblk_ok"], b + 1)
                else:
                    pe.wait_ge(s["kblk_p"], b - G + 1)
                if i % 4 == 0:
                    pe.wait_ge(s["qh_out"], i // 4 + 1)
                if i >= 2:
                    pe.wait_ge(s["ssub_ok"], i - 1)
                mm(bank[3 + i % 2][:, :], qh[:, i * P:(i + 1) * P], k_blk[:, b].rearrange("p h q -> p (h q)")).then_inc(s["s_mm"], 1)

            def transpose_scores(i):
                pe.wait_ge(s["ssub_ok"], i + 1)
                if i == 0:
                    pe.wait_ge(s["qh_out"], 2)
                if i >= 2:
                    pe.wait_ge(s["exp_ok"], i - 1)
                for j in range(PAIRS):
                    m = pe.transpose(bank[5 + i % 2][:, j * P:(j + 1) * P],
                                     s_sub[:, i % 2, 2 * j:2 * j + 2].rearrange("p h q -> p (h q)"), w("ident"))
                m.then_inc(s["pt_mm"], 1)

            def value_tile(i):
                b = i // S
                pe.wait_ge(s["exp_ok"], i + 1)
                pe.wait_ge(s["v_even"], b // G + 1)
                pe.wait_ge(s["v_odd"], b // G + 1)
                if i >= 1:
                    pe.wait_ge(s["att_ok"], i)
                for j in range(PAIRS):
                    m = mm(bank[7][:, j * VW:(j + 1) * VW], p_t[:, i % 2, j], v_blk[:, b, j])
                m.then_inc(s["av_mm"], 1)

            def att_transpose(i):
                pe.wait_ge(s["att_ok"], i + 1)
                if i >= 1:
                    pe.wait_ge(s["attt_ok"], i)
                pe.transpose(bank[0][:, 0:P], att[:, i % 2], w("ident")).then_inc(s["attt_mm"], 1)

            def out_project(i):
                pe.wait_ge(s["attt_ok"], i + 1)
                if i >= 1:
                    pe.wait_ge(s["z_ok"], i)
                mm(bank[1][:, 0:C], att_t[:, i % 2], w("mo_w")).then_inc(s["msa_mm"], 1)

            def z_transpose(b):
                pe.wait_ge(s["zhat_ok"], 2 * b + 2)
                if b == 0:
                    pe.wait_ge(s["out_bias_ok"], 1)
                if b >= 1:
                    pe.wait_ge(s["zt_ok"], b)
                for t in range(S):
                    m = pe.transpose(bank[2][:, t * P:(t + 1) * P], z_hat[:, 2 * b + t], w("ident"))
                m.then_inc(s["zt_mm"], 1)

            def fold_late():
                pe.wait_ge(s["k_out"], 2)
                pe.wait_ge(s["late_in"], 16)
                mm(bank[2][0:1, C:2 * C], w("ln_b"), w("mlp_w"), stop=False)
                mm(bank[2][0:1, C:2 * C], ones_row[:, 0:1], r("mlp_b"), start=False)
                mm(bank[2][:, 0:C], w("wv1T"), w("wo1"))
                mm(bank[2][:, 2 * C:2 * C + 1], w("wq1"), w("gn_beta"))
                mm(bank[2][:, 2 * C + 1:2 * C + 2], w("wk1"), w("gn_beta")).then_inc(s["fold3"], 1)

            def out_bias_rows():
                pe.wait_ge(s["mlp_row_ok"], 1)
                pe.wait_ge(s["fold3_out"], 1)
                pe.wait_ge(s["cols1_ok"], 2)
                mm(bank[2][:, 0:C], w("bv1").to_broadcast([P, P]), w("wo1"), stop=False)
                mm(bank[2][:, 0:C], w("gn_beta").to_broadcast([P, P]), w_vo[:, :], start=False, stop=False)
                mm(bank[2][:, 0:C], ones_row[:, :], r("bo1"), start=False).then_inc(s["out_bias_mm"], 1)

            score_tile(0)
            score_tile(1)
            key_half(1)
            for i in range(T + 1):
                if i < T:
                    transpose_scores(i)
                if i == 1:
                    fold_late()
                if i >= 1:
                    value_tile(i - 1)
                if i == 2:
                    out_bias_rows()
                if i >= 2:
                    out_project(i - 2)
                if i + 2 < T:
                    score_tile(i + 2)
                if i >= 6 and i % 2 == 0:
                    z_transpose((i - 6) // 2)
                if i >= 1:
                    att_transpose(i - 1)

            def mlp_image(b):
                pe.wait_ge(s["zt_ok"], b + 1)
                pe.wait_ge(s["mlp_wg_ok"], 1)
                pe.wait_ge(s["mlp_row_ok"], 1)
                for t in range(S):
                    i = 2 * b + t
                    o = bank[3 + b][:, t * C:(t + 1) * C]
                    mm(o, ones_row[:, :], mlp_row[:, :], stop=False)
                    m = mm(o, z_t[:, i], mlp_wg[:, :], start=False)
                m.then_inc(s["mlp_mm"], 1)

            def x1_transpose(b):
                pe.wait_ge(s["x1_ok"], b + 1)
                for t in range(S):
                    m = pe.transpose(bank[3 + b][:, t * P:(t + 1) * P], x1[:, 2 * b + t], w("ident"))
                m.then_inc(s["x1t_mm"], 1)

            def gn_set(n):
                i = slice(GN_SETS[n].start, GN_SETS[n].stop)
                k = i.stop - i.start
                pe.wait_ge(s["gmv_ok"], i.stop)
                if n == 1:
                    pe.wait_ge(s["v1_ok"], 1)
                mm(bank[7][:, 0:k], w("group_mean"), gmv[:, i, 0]).then_inc(s["gm_mm"], 1)
                pe.wait_ge(s["spread_ok"], n + 1)
                mm(bank[7][:, B:B + k], w("group_mean"), spread[:, i]).then_inc(s["gv_mm"], 1)

            def project_qk(b):
                wait_xgn(pe, b)
                pe.wait_ge(s["gamma_ok"], 1)
                if b >= 2:
                    pe.wait_ge(s["k1_ok"], b - 1)
                mm(bank[b % 2][:, 0:HW], wq1g[:, :], x_gn[:, b])
                mm(bank[b % 2][:, HW:2 * HW], wk1g[:, :], x_gn[:, b]).then_inc(s["qk_mm"], 1)

            def project_v(b):
                if b == 0:
                    pe.wait_ge(s["gve_ok"], 1)
                else:
                    pe.wait_ge(s["v1_ok"], b)
                if b == 1:
                    pe.wait_ge(s["gve_ok"], 2)
                for t in range(S):
                    m = mm(bank[7][:, t * C:(t + 1) * C], x_gn[:, b, t * P:(t + 1) * P], w_vog[:, :])
                m.then_inc(s["v1_mm"], 1)

            def score_image(b):
                pe.wait_ge(s["q1_ok"], b + 1)
                pe.wait_ge(s["k1_ok"], b + 1)
                if b < 2:
                    wait_xgn(pe, b)
                else:
                    pe.wait_ge(s["p1_ok"], 2 * (b - 1))
                for t in range(S):
                    m = mm(bank[3 + b % 2][:, t * HW:(t + 1) * HW], q1[:, b, t * P:(t + 1) * P], k1[:, b])
                m.then_inc(s["s1_mm"], 1)

            def transpose_image(b):
                pe.wait_ge(s["p1_ok"], 2 * b + 2)
                if b == 0:
                    wait_xgn(pe, 2)
                else:
                    pe.wait_ge(s["p1t_ok"], b)
                for t in range(S):
                    for j in range(S):
                        o = (t * S + j) * P
                        m = pe.transpose(bank[5][:, o:o + P], p1[:, b % 2, t, j * P:(j + 1) * P], w("ident"))
                m.then_inc(s["p1t_mm"], 1)

            def value_image(b):
                pe.wait_ge(s["p1t_ok"], b + 1)
                pe.wait_ge(s["v1_ok"], b + 1)
                pe.wait_ge(s["v1ones_set"], 1)
                if b >= 1:
                    pe.wait_ge(s["y_ok"], 2 * b)
                for t in range(S):
                    for j in range(S):
                        m = mm(bank[2][:, t * HW:t * HW + C + 1], p1_t[:, b % 2, t, j], v1[:, b, j], start=(j == 0), stop=(j == S - 1))
                    m.then_inc(s["av1_mm"], 1)

            mlp_image(0)
            out_project(T - 1)
            mlp_image(1)
            z_transpose(2)
            x1_transpose(0)
            x1_transpose(1)
            mlp_image(2)
            z_transpose(3)
            x1_transpose(2)
            gn_set(0)
            mlp_image(3)
            project_qk(0)
            project_v(0)
            project_qk(1)
            x1_transpose(3)
            score_image(0)
            gn_set(1)
            project_v(1)
            project_qk(2)
            score_image(1)
            transpose_image(0)
            project_v(2)
            value_image(0)
            project_qk(3)
            score_image(2)
            transpose_image(1)
            project_v(3)
            value_image(1)
            score_image(3)
            transpose_image(2)
            value_image(2)
            transpose_image(3)
            value_image(3)


def kernel(**inputs):
    import numpy as np
    import concourse.bacc as bacc
    from concourse.bass_utils import run_bass_kernel_spmd as run

    get = {k: np.asarray(v) for k, v in inputs.items()}
    L0, L1 = "L0_conv_", "L1_conv_"
    p = np.arange(P)
    f32 = np.float32

    const = {
        "ident": np.eye(P, dtype=f32),
        "head_of": (p[:, None] // HD == np.arange(NH)[None, :]).astype(f32),
        "ones_mask": (p[:, None] // PIX == np.arange(2)[None, :]).astype(f32),
        "group_mean": ((p[:, None] // GROUP == p[None, :] // GROUP) / GROUP).astype(f32),
    }
    half = np.arange(OH) + 0.5
    centre = ((half * (2.0 / OH)) * (H / R) / 2.0 + 1.0) * 0.5 * (W - 1)
    const["grid_x"] = (np.tile(centre, G * OH)[None, :] - (p % W)[:, None]).astype(f32)
    const["grid_y"] = np.concatenate([np.tile(np.repeat(centre, OW), G)[None, :] - (t * (P // W) + p // W)[:, None]
                                      for t in range(S)], axis=1).astype(f32)

    col = lambda a: a.reshape(C, 1)
    conv_order = lambda a: a.reshape(-1, OH // 2, 2, OW, 2).transpose(0, 2, 1, 4, 3).reshape(-1, C)
    data = {
        "dw_w": get[L0 + "dw_w"].reshape(C, KS * KS), "pw": get[L0 + "pw_w"].reshape(2, C).T,
        "wq_conv": conv_order(get[L0 + "wq"]), "wqT": get[L0 + "wq"].T, "wvT": get[L0 + "wv"].T,
        "wv1T": get[L1 + "wv"].T, "wo1": get[L1 + "wo"], "wq1": get[L1 + "wq"], "wk1": get[L1 + "wk"],
        "bq1": col(get[L1 + "bq"]), "bk1": col(get[L1 + "bk"]), "bv1": col(get[L1 + "bv"]),
        "gn_gamma": col(get[L1 + "gn_gamma"]), "gn_beta": col(get[L1 + "gn_beta"]),
    }
    for n in ("dw_b", "bq", "mq_b", "bv", "mk_b", "mv_b", "ln_g", "ln_b"):
        data[n] = col(get[L0 + n])
    for n in ("mq_w", "mk_w", "mv_w", "mo_w", "mlp_w"):
        data[n] = get[L0 + n]
    row = {"ln_b": get[L0 + "ln_b"].reshape(1, C), "bq_conv": conv_order(get[L0 + "bq"].reshape(1, C)), "mo_b": get[L0 + "mo_b"].reshape(1, C),
           "mlp_b": get[L0 + "mlp_b"].reshape(1, C), "bo1": get[L1 + "bo"].reshape(1, C)}

    arrays = {
        "x": np.ascontiguousarray(get["x"]).reshape(B, HW, C),
        **{pack: np.ascontiguousarray(np.concatenate([const[n] if n in const else data[n] for n, _ in parts], axis=1))
           for pack, parts in PACKS.items()},
        "rows": np.ascontiguousarray(np.concatenate([row[n] for n in ROWS], axis=1)),
        "ln_rows": np.ascontiguousarray(np.concatenate([get[L0 + "ln_g"], get[L0 + "ln_b"]])),
    }
    nc = bacc.Bacc("TRN2", target_bir_lowering=False, num_devices=1)
    args = [nc.dram_tensor(n, a.shape, mybir.dt.from_np(a.dtype), kind="ExternalInput").ap() for n, a in arrays.items()]
    out = nc.dram_tensor("out", (B, HW, C), F32, kind="ExternalOutput").ap()
    build(nc, *args, out)
    got = run(nc, [arrays], core_ids=[0]).results[0]["out"]
    return got.reshape(B, H, W, C)
```

```python
from contextlib import ExitStack

import concourse.bass as bass
from concourse import mybir
from concourse.alu_op_type import AluOpType as ALU

F32 = mybir.dt.float32
BF16 = mybir.dt.bfloat16
ACT = mybir.ActivationFunctionType
AX = mybir.AxisListType

P = 128
B, H, W, C = 4, 16, 16, 128
HW = H * W
S = HW // P
T = B * S
NH = 8
HD = C // NH
G = 2
PAIRS = NH // 2
KS, R = 7, 2
OH, OW = H // R, W // R
PIX = OH * OW
VW = 2 * HD + 2
LN_EPS, GN_EPS = 1e-5, 1e-6
GROUP = C // 32
N_PE, N_POOL = 17, 11
N_DIAG_DVE, N_DIAG_POOL = 1, 6
N_WARM = 8

PACKS = {
    "early": [("dw_w", KS * KS), ("ln_g", 1), ("ln_b", 1), ("pw", 2), ("dw_b", 1), ("bq", 1), ("mq_b", 1), ("bv", 1),
              ("mk_b", 1), ("mv_b", 1), ("gn_gamma", 1), ("gn_beta", 1), ("bq1", 1), ("bk1", 1), ("bv1", 1), ("mlp_b", 1),
              ("ident", P), ("wq_conv", C)],
    "fold": [("wqT", C), ("mq_w", C), ("wvT", C), ("mk_w", C), ("mv_w", C)],
    "mid": [("mo_w", C), ("head_of", NH), ("ones_mask", 2), ("grid_x", G * PIX), ("grid_y", S * G * PIX)],
    "late": [("mlp_w", C), ("wv1T", C), ("wo1", C), ("wq1", C), ("wk1", C), ("group_mean", P), ("group_rest", P)],
}
ROWS = ["bq_conv", "ln_b", "mo_b", "bo1"]


def columns(parts):
    at, out = 0, {}
    for name, n in parts:
        out[name] = (at, at + n)
        at += n
    return out, at


PLACE = {pack: columns(parts) for pack, parts in PACKS.items()}


def tap_range(k, n):
    shift, phase = divmod(k - KS // 2, R)
    return phase, shift, max(0, -shift), min(n, n - shift)


def reach(tap):
    n = 1
    for k, size in zip(tap, (OH, OW)):
        _, _, a, b = tap_range(k, size)
        n *= b - a
    return n


def share_taps():
    first = {"pe": (3, 3), "dve0": (4, 4), "dve1": (3, 4), "pool": (4, 3)}
    taps = [(ky, kx) for ky in range(KS) for kx in range(KS)]
    rest = sorted((t for t in taps if t not in first.values()), key=reach)
    pool, rest = rest[:N_POOL - 1], rest[N_POOL - 1:]
    pe, dve = rest[:N_PE - 1], rest[N_PE - 1:]
    return [first["pe"]] + pe, [first["dve0"], first["dve1"]] + dve, [first["pool"]] + pool


PE_TAPS, DVE_TAPS, POOL_TAPS = share_taps()


def build(nc, x, early, fold, mid, late, rows, ln_rows, out):
    ctx = ExitStack()
    with ctx:
        def sb(name, shape, dt=F32):
            return ctx.enter_context(nc.sbuf_tensor(name, shape, dt))

        def sem(name):
            return ctx.enter_context(nc.semaphore(name))

        bank = [ctx.enter_context(nc.psum_tensor(f"bank{i}", [P, 512], F32)) for i in range(8)]

        x_hw = sb("x_hw", [P, T, C])
        x_st = sb("x_st", [P, B, S * C])
        packs = {n: sb(f"pack_{n}", [P, PLACE[n][1]]) for n in PACKS}
        row = sb("row", [1, len(ROWS) * C])
        gb = sb("gb", [P, 2 * C])
        ones_row = sb("ones_row", [1, P])
        ones_col = sb("ones_col", [P, 1])
        warm = sb("warm", [P, P], BF16)
        eps = sb("eps", [P, 1])
        scratch = sb("scratch", [P, 3])
        neg_half = sb("neg_half", [P, B])

        def w(name):
            for n, (at, _) in PLACE.items():
                if name in at:
                    return packs[n][:, at[name][0]:at[name][1]]
            raise KeyError(name)

        def r(name):
            i = ROWS.index(name)
            return row[:, i * C:(i + 1) * C]

        st = sb("st", [P, T, 6])
        mv = sb("mv", [P, T, 2])
        sd = sb("sd", [P, T])
        rstd = sb("rstd", [P, T])
        shift = sb("shift", [P, 4])
        x_hat = sb("x_hat", [P, T, C])
        x_g = sb("x_g", [P, T, C])
        x_ln = sb("x_ln", [P, T, C])
        colsum = sb("colsum", [1, C])
        q_bias = sb("q_bias", [P, HW])
        m_q = sb("m_q", [P, C])
        m_kv = sb("m_kv", [P, 2 * C])
        w_vo = sb("w_vo", [P, C])
        cols = sb("cols", [P, 3])
        cols1 = sb("cols1", [P, 3])
        wq1g = sb("wq1g", [P, C])
        wk1g = sb("wk1g", [P, C])
        w_vog = sb("w_vog", [P, C])
        mlp_wg = sb("mlp_wg", [P, C])
        msa_bias = sb("msa_bias", [P, C])
        out_bias = sb("out_bias", [P, C])
        x_res = sb("x_res", [P, T, C])
        diag = sb("diag", [P, len(PE_TAPS), P])
        q_conv = sb("q_conv", [P, 2 * OH * B * 2 * OW])
        acc = sb("acc", [P, 4, OH * B * OW])
        prod = sb("prod", [P, len(POOL_TAPS), OH * B * OW])
        o_act = sb("o_act", [P, B, OH, OW])
        qh = sb("qh", [P, T * P])
        tanh = sb("tanh", [P, 2, 2, G * PIX])
        dist_x = sb("dist_x", [P, 2, G * PIX])
        dist_y = sb("dist_y", [P, 2, S, G * PIX])
        falling_x = sb("falling_x", [P, 2, G * PIX])
        abs_y = sb("abs_y", [P, 2, S * G * PIX])
        hat_x = sb("hat_x", [P, 2, G * PIX])
        hat_y = sb("hat_y", [P, 2, S, G * PIX])
        bilin = sb("bilin", [P, 2, S, G * PIX])
        sampled = sb("sampled", [P, B, PIX])
        k_t = sb("k_t", [P, B, PIX])
        k_blk = sb("k_blk", [P, B, NH, PIX])
        v_blk = sb("v_blk", [P, B, PAIRS, VW])
        smax = sb("smax", [P, 2, NH])
        s_sub = sb("s_sub", [P, 2, NH, PIX])
        p_t = sb("p_t", [P, 2, PAIRS, P])
        recip = sb("recip", [P, 2, NH])
        att = sb("att", [P, 2, C])
        att_t = sb("att_t", [P, 2, P])
        z = sb("z", [P, T, C])
        zst = sb("zst", [P, T, 6])
        zmv = sb("zmv", [P, T, 2])
        zve = sb("zve", [P, T])
        zrs = sb("zrs", [P, T])
        z_hat = sb("z_hat", [P, T, C])
        z_t = sb("z_t", [P, T, P])
        gel_t = sb("gel_t", [P, B, HW])
        x1_t = sb("x1_t", [P, B, HW])
        z_res = sb("z_res", [P, T, C])
        x1_res = sb("x1_res", [P, T, C])
        gst = sb("gst", [P, B, 6])
        gmv = sb("gmv", [P, B, 2])
        gmean = sb("gmean", [P, B])
        dev2 = sb("dev2", [P, B])
        gve = sb("gve", [P, B])
        grs = sb("grs", [P, B])
        x_gn = sb("x_gn", [P, B, HW])
        q1 = sb("q1", [P, B, HW])
        k1 = sb("k1", [P, B, HW])
        v1 = sb("v1", [P, B, S, C + 1])
        nmax1 = sb("nmax1", [P, T])
        p1 = sb("p1", [P, 2, S, HW])
        p1_t = sb("p1_t", [P, 2, S, S, P])
        rec1 = sb("rec1", [P, T])
        y = sb("y", [P, T, C])

        stages = {
            "loads and constants": """x_in0 x_in1 x_in2 early_in fold_in mid_in late_in rows_in lnrow_in xst_in
                warm_set ones_set consts acc_set vones_set v1ones_set""",
            "norm of x": "stats aggr sdev rstd_ok shift_ok hat_ok hat_a xg_ok xln_ok",
            "folded weights": """colsum_mm colsum_ok qbias_mm qbias_ok foldq_mm m_q_ok cols_ok foldkv_mm m_kv_ok
                fold1_mm w_vo_ok cols1_ok outbias_mm outbias_ok msabias_mm msabias_ok mlpw_ok gamma_ok""",
            "convolution": """q_mm q_out diag_a diag_v diag_p acc0_ok acc1_ok prod_ok accp0_ok accp1_ok conv_mm gelu_ok""",
            "sampling": "coord_mm tanh_ok dx_ok dy_ok fx_ok ay_ok hx_ok hy_ok bilin_ok interp_mm sampled_ok",
            "queries, keys, values": "qh_mm qh_ok k_mm k_ok kblk_ok kblk_p v_mm v_even v_odd",
            "attention": """s_mm smax_ok ssub_ok pt_mm exp_ok av_mm recip_ok att_ok attt_mm attt_ok msa_mm xres_ok z_ok""",
            "norm of z and MLP": "zst_ok zmv_ok zve_ok zrs_ok zhat_ok zt_mm zt_ok mlp_mm gel_ok zres_ok x1t_ok gelt_mm x1res_ok",
            "group norm": "gst_ok gmv_ok dev_mm dev2_ok gvar_mm gve_ok gmean_ok grs_ok xgn_ok",
            "second attention": """qk_mm q1_ok k1_ok v1_mm v1_ok s1_mm nmax1_ok p1_ok p1t0_mm p1t1_mm p1t0_ok p1t1_ok
                av1_mm rec1_ok y_ok y_out""",
        }
        s = {n: sem(n) for group in stages.values() for n in group.split()}

        block = ctx.enter_context(nc.Block())

        x_hw_dram = x.rearrange("b (s p) c -> p b s c", p=P)
        x_st_dram = x.rearrange("b (p s) c -> p b (s c)", s=S)
        out_dram = out.rearrange("b (p s) c -> p b (s c)", s=S)

        def halves(h):
            return slice(4 * h, 4 * h + 4)

        def tap_views(tap, dst):
            ry, ay, y0, y1 = tap_range(tap[0], OH)
            rx, ax, x0, x1_ = tap_range(tap[1], OW)
            src = q_conv[:, :].rearrange("c (r yb t x) -> c r yb t x", r=2, t=2, x=OW)[
                :, ry, B * (y0 + ay):B * (y1 + ay), rx, x0 + ax:x1_ + ax]
            return src, dst.rearrange("c (yb x) -> c yb x", x=OW)[:, B * y0:B * y1, x0:x1_]

        def tap_weight(tap):
            i = tap[0] * KS + tap[1]
            return w("dw_w")[:, i:i + 1]

        DVE_D = list(range(0, N_DIAG_DVE))
        POOL_D = list(range(len(PE_TAPS) - N_DIAG_POOL, len(PE_TAPS)))
        ACT_D = [i for i in range(len(PE_TAPS)) if i not in DVE_D + POOL_D]

        GN_SETS = [range(0, 2), range(2, 4)]

        def value_half(copy, eng, e, g, done):
            h = slice(e * PIX, (e + 1) * PIX)
            eng.wait_ge(s["v_mm"], g + 1)
            eng.wait_ge(s["vones_set"], 1)
            copy(v_blk[h, 2 * g:2 * g + 2, :, e * HD:(e + 1) * HD].rearrange("p b j d -> p (b j) d"),
                 bank[g][h, 0:G * PAIRS * HD].rearrange("p (n d) -> p n d", d=HD)).then_inc(done, 1)

        def query_image(b):
            at = HW if b == 1 else 0
            return bank[max(b - 1, 0)][:, at:at + HW]

        def probs_out(copy, eng, b, t):
            eng.wait_ge(s[f"p1t{t}_mm"], b + 1)
            if b >= 2:
                eng.wait_ge(s["av1_mm"], 2 * (b - 2) + t + 1)
            copy(p1_t[:, b % 2, t].rearrange("p j q -> p (j q)"), bank[(2, 0)[t]][:, 0:HW]).then_inc(s[f"p1t{t}_ok"], 1)

        def av_bank(b, t):
            return bank[{(2, 1): 1, (3, 0): 3, (3, 1): 4}.get((b, t), 7)]

        def zt_bank(b):
            return bank[2 if b % 2 == 0 else 7]

        @block.sync
        def _(sp):
            for b in range(G):
                sp.dma_start(x_hw[:, S * b:S * b + S, :], x_hw_dram[:, b]).then_inc(s[f"x_in{b}"], 16)
            sp.dma_start(packs["early"][:, :], early).then_inc(s["early_in"], 16)
            sp.dma_start(row[:, :], rows).then_inc(s["rows_in"], 16)
            sp.dma_start(x_hw[:, halves(1), :].rearrange("p (b s) c -> p b s c", s=S), x_hw_dram[:, G:B]).then_inc(s["x_in2"], 16)
            sp.dma_start(packs["fold"][:, :], fold).then_inc(s["fold_in"], 16)
            sp.dma_start(gb[:, :], ln_rows.partition_broadcast(P)).then_inc(s["lnrow_in"], 16)
            sp.dma_start(packs["mid"][:, :], mid).then_inc(s["mid_in"], 16)
            sp.dma_start(x_st[:, :, :], x_st_dram).then_inc(s["xst_in"], 16)
            sp.dma_start(packs["late"][:, :], late).then_inc(s["late_in"], 16)
            for b in range(B - 1):
                sp.wait_ge(s["y_ok"], 2 * b + 2)
                sp.dma_start(out_dram[:, b, :], y[:, 2 * b:2 * b + 2, :].rearrange("p s c -> p (s c)")).then_inc(s["y_out"], 16)
            for i in (T - 2, T - 1):
                sp.wait_ge(s["y_ok"], i + 1)
                t = i % S
                sp.dma_start(out_dram[:, B - 1, t * C:(t + 1) * C], y[:, i, :]).then_inc(s["y_out"], 16)
            sp.wait_ge(s["y_out"], 16 * (B + 1))

        @block.gpsimd
        def _(pool):
            pool.memset(warm[:, :], 0.0).then_inc(s["warm_set"], 1)
            pool.memset(ones_row[:, :], 1.0)
            pool.memset(ones_col[:, :], 1.0).then_inc(s["ones_set"], 1)
            pool.memset(eps[:, :], LN_EPS)
            pool.memset(neg_half[:, :], -0.5).then_inc(s["consts"], 1)
            pool.memset(acc[:, 3, :], 0.0).then_inc(s["acc_set"], 1)
            pool.memset(v1[:, :, :, C:C + 1], 1.0).then_inc(s["v1ones_set"], 1)
            pool.memset(v_blk[:, :, :, 0:2 * HD], 0.0)
            pool.wait_ge(s["early_in"], 16)
            for i in POOL_D[:3]:
                pool.tensor_scalar(diag[:, i, :], w("ident"), tap_weight(PE_TAPS[i]), None, ALU.mult).then_inc(s["diag_p"], 1)

            def norm_affine(h):
                t = halves(h)
                pool.wait_ge(s["hat_ok"], (4, 6)[h])
                if h == 1:
                    pool.wait_ge(s["hat_a"], 2)
                pool.wait_ge(s["lnrow_in"], 16)
                pool.tensor_tensor(x_g[:, t], x_hat[:, t], gb[:, 0:C].unsqueeze(1).to_broadcast([P, 4, C]), ALU.mult).then_inc(s["xg_ok"], 1)
                pool.wait_ge(s["xg_ok"], h + 1)
                pool.tensor_tensor(x_ln[:, t], x_g[:, t], gb[:, C:2 * C].unsqueeze(1).to_broadcast([P, 4, C]), ALU.add).then_inc(s["xln_ok"], 1)

            norm_affine(0)
            for i in POOL_D[3:]:
                pool.tensor_scalar(diag[:, i, :], w("ident"), tap_weight(PE_TAPS[i]), None, ALU.mult).then_inc(s["diag_p"], 1)
            for n, tap in enumerate(POOL_TAPS):
                if n == 0:
                    continue
                chain, k = n % 2, n // 2
                _, dst = tap_views(tap, acc[:, 2 + chain, :])
                _, src = tap_views(tap, prod[:, n, :])
                pool.wait_ge(s["prod_ok"], n + 1)
                if n == 1:
                    pool.wait_ge(s["acc_set"], 1)
                if n >= 3:
                    pool.wait_ge(s[f"accp{chain}_ok"], k - 1 + chain)
                pool.tensor_tensor(dst, dst, src, ALU.add).then_inc(s[f"accp{chain}_ok"], 1)
            norm_affine(1)
            pool.wait_ge(s["mid_in"], 16)
            pool.tensor_copy(v_blk[:, :, :, 2 * HD:VW],
                             w("ones_mask").unsqueeze(1).unsqueeze(1).to_broadcast([P, B, PAIRS, 2])).then_inc(s["vones_set"], 1)
            pool.wait_ge(s["msabias_ok"], 1)
            pool.wait_ge(s["xst_in"], 16)
            pool.tensor_tensor(x_res[:, :, :], x_st[:, :, :].rearrange("p b (s c) -> p (b s) c", s=S),
                               msa_bias[:, :].unsqueeze(1).to_broadcast([P, T, C]), ALU.add).then_inc(s["xres_ok"], 1)
            for b in range(G, B):
                pool.wait_ge(s["k_ok"], 1)
                pool.tensor_tensor(k_blk[:, b], k_t[:, b].unsqueeze(1).to_broadcast([P, NH, PIX]),
                                   w("head_of").unsqueeze(2).to_broadcast([P, NH, PIX]), ALU.mult).then_inc(s["kblk_p"], 1)
            pool.wait_ge(s["late_in"], 16)
            pool.tensor_scalar(mlp_wg[:, :], w("mlp_w"), w("ln_g"), None, ALU.mult).then_inc(s["mlpw_ok"], 1)

            def z_scale(b):
                pool.wait_ge(s["zve_ok"], b + 1)
                pool.tensor_tensor(zrs[:, 2 * b:2 * b + 2], zve[:, 2 * b:2 * b + 2], neg_half[:, 0:2], ALU.pow).then_inc(s["zrs_ok"], 1)

            def residual(b):
                pool.wait_ge(s["z_ok"], 2 * b + 2)
                pool.wait_ge(s["outbias_ok"], 1)
                pool.tensor_tensor(z_res[:, 2 * b:2 * b + 2, :], z[:, 2 * b:2 * b + 2, :],
                                   out_bias[:, :].unsqueeze(1).to_broadcast([P, S, C]), ALU.add).then_inc(s["zres_ok"], 1)

            def gn_pow(n):
                i = slice(GN_SETS[n].start, GN_SETS[n].stop)
                pool.wait_ge(s["gve_ok"], n + 1)
                pool.tensor_tensor(grs[:, i], gve[:, i], neg_half[:, i], ALU.pow).then_inc(s["grs_ok"], 1)

            z_scale(0)
            pool.tensor_scalar(wq1g[:, :], w("wq1"), w("gn_gamma"), None, ALU.mult)
            pool.tensor_scalar(wk1g[:, :], w("wk1"), w("gn_gamma"), None, ALU.mult)
            pool.wait_ge(s["w_vo_ok"], 1)
            pool.tensor_scalar(w_vog[:, :], w_vo[:, :], w("gn_gamma"), None, ALU.mult).then_inc(s["gamma_ok"], 1)
            z_scale(1)
            residual(0)
            residual(1)
            z_scale(2)
            z_scale(3)
            gn_pow(0)
            residual(2)
            residual(3)
            gn_pow(1)

        @block.scalar
        def _(act):
            act.wait_ge(s["consts"], 1)
            act.activation(scratch[:, 0:1], eps[:, :], ACT.Sqrt)

            def diagonals(which):
                for i in which:
                    act.activation(diag[:, i, :], w("ident"), ACT.Copy, scale=tap_weight(PE_TAPS[i])).then_inc(s["diag_a"], 1)

            act.wait_ge(s["aggr"], 4)
            act.activation(sd[:, halves(0)], mv[:, halves(0), 1], ACT.Sqrt, bias=eps[:, 0:1]).then_inc(s["sdev"], 1)
            act.wait_ge(s["early_in"], 16)
            diagonals(ACT_D[:8])
            act.wait_ge(s["aggr"], 8)
            act.activation(sd[:, halves(1)], mv[:, halves(1), 1], ACT.Sqrt, bias=eps[:, 0:1]).then_inc(s["sdev"], 1)
            act.wait_ge(s["qbias_mm"], 1)
            act.copy(q_bias[:, :].rearrange("c (r s n) -> c r s n", r=2, s=S),
                     bank[5][:, 0:C].rearrange("c (r n) -> c r n", r=2).unsqueeze(2).to_broadcast([P, 2, S, C // 2])).then_inc(s["qbias_ok"], 1)
            act.wait_ge(s["shift_ok"], 1)
            for i in range(6, T):
                act.activation(x_hat[:, i], x_hw[:, i], ACT.Identity, scale=rstd[:, i:i + 1],
                               bias=shift[:, i - 4:i - 3]).then_inc(s["hat_a"], 1)
            diagonals(ACT_D[8:])
            act.wait_ge(s["q_out"], B)
            for n, tap in enumerate(POOL_TAPS):
                src, dst = tap_views(tap, acc[:, 2, :] if n == 0 else prod[:, n, :])
                act.activation(dst, src, ACT.Copy, scale=tap_weight(tap)).then_inc(s["prod_ok"], 1)
            act.wait_ge(s["foldq_mm"], 1)
            act.copy(m_q[:, :], bank[6][:, 0:C]).then_inc(s["m_q_ok"], 1)
            for j, name in enumerate(("mq_b", "mk_b", "mv_b")):
                act.activation(cols[:, j:j + 1], bank[6][:, C + j:C + j + 1], ACT.Identity,
                               bias=w(name)).then_inc(s["cols_ok"], 1)
            act.wait_ge(s["foldkv_mm"], 1)
            act.copy(m_kv[:, :], bank[7][:, 0:2 * C]).then_inc(s["m_kv_ok"], 1)
            act.wait_ge(s["conv_mm"], 1)
            act.activation(o_act[:, :, :, :].rearrange("c b y x -> c y b x"),
                           bank[3][:, 0:B * PIX].rearrange("c (y b x) -> c y b x", b=B, x=OW), ACT.Gelu, bias=w("dw_b")).then_inc(s["gelu_ok"], 1)
            for g in range(2):
                act.wait_ge(s["coord_mm"], g + 1)
                act.activation(tanh[:, g].rearrange("p d q -> p (d q)"), bank[7 - g][:, 0:2 * G * PIX], ACT.Tanh).then_inc(s["tanh_ok"], 1)
            for g in range(2):
                act.wait_ge(s["dy_ok"], g + 1)
                act.activation(abs_y[:, g], dist_y[:, g].rearrange("p s q -> p (s q)"), ACT.Abs).then_inc(s["ay_ok"], 1)
                act.wait_ge(s["ay_ok"], g + 1)
                act.activation(hat_y[:, g].rearrange("p s q -> p (s q)"), abs_y[:, g], ACT.Relu, scale=-1.0, bias=1.0).then_inc(s["hy_ok"], 1)
                if g == 0:
                    act.wait_ge(s["cols_ok"], 3)
                    act.wait_ge(s["qh_mm"], 1)
                    act.activation(qh[:, 0:512], bank[4][:, :], ACT.Identity, bias=cols[:, 0:1]).then_inc(s["qh_ok"], 1)
            act.wait_ge(s["msabias_mm"], 1)
            act.copy(msa_bias[:, :], bank[6][:, 0:C]).then_inc(s["msabias_ok"], 1)
            act.activation(scratch[:, 1:2], eps[:, :], ACT.Exp)
            act.wait_ge(s["fold1_mm"], 1)
            act.copy(w_vo[:, :], bank[7][:, 0:C]).then_inc(s["w_vo_ok"], 1)
            for j, name in enumerate(("bq1", "bk1", "mlp_b")):
                act.activation(cols1[:, j:j + 1], bank[7][:, C + j:C + j + 1], ACT.Identity, bias=w(name)).then_inc(s["cols1_ok"], 1)
            value_half(act.copy, act, 1, 0, s["v_odd"])
            act.wait_ge(s["qh_mm"], 2)
            act.activation(qh[:, 512:1024], bank[5][:, :], ACT.Identity, bias=cols[:, 0:1]).then_inc(s["qh_ok"], 1)
            act.wait_ge(s["k_mm"], 2)
            act.activation(k_t[:, G:B, :].rearrange("c b q -> c (b q)"), bank[2][:, 0:G * PIX], ACT.Identity,
                           bias=cols[:, 1:2]).then_inc(s["k_ok"], 1)
            value_half(act.copy, act, 1, 1, s["v_odd"])

            def exp_tile(i):
                act.wait_ge(s["pt_mm"], i + 1)
                if i >= 2:
                    act.wait_ge(s["av_mm"], i - 1)
                act.activation(p_t[:, i % 2].rearrange("p j q -> p (j q)"), bank[5 + i % 2][:, :], ACT.Exp).then_inc(s["exp_ok"], 1)

            def att_tile(i):
                act.wait_ge(s["attt_mm"], i + 1)
                if i >= 2:
                    act.wait_ge(s["msa_mm"], i - 1)
                act.copy(att_t[:, i % 2], bank[0][:, 0:P]).then_inc(s["attt_ok"], 1)

            def zt_image(b):
                act.wait_ge(s["zt_mm"], b + 1)
                act.copy(z_t[:, 2 * b:2 * b + 2, :].rearrange("c s q -> c (s q)"), zt_bank(b)[:, 0:HW]).then_inc(s["zt_ok"], 1)

            def gelu_image(b):
                act.wait_ge(s["mlp_mm"], b + 1)
                act.activation(gel_t[:, b], bank[3 + b][:, 0:HW], ACT.Gelu, bias=cols1[:, 2:3]).then_inc(s["gel_ok"], 1)

            for i in range(T - 1):
                if i >= 2:
                    att_tile(i - 2)
                exp_tile(i)
            act.wait_ge(s["outbias_mm"], 1)
            act.copy(out_bias[:, :], bank[7][:, 0:C]).then_inc(s["outbias_ok"], 1)
            exp_tile(T - 1)
            att_tile(T - 3)
            zt_image(0)
            act.activation(scratch[:, 2:3], eps[:, :], ACT.Gelu)
            zt_image(1)
            att_tile(T - 2)
            act.wait_ge(s["cols1_ok"], 3)
            gelu_image(0)
            gelu_image(1)
            att_tile(T - 1)
            zt_image(2)
            gelu_image(2)
            zt_image(3)
            gelu_image(3)

            def value_copy(b):
                act.wait_ge(s["v1_mm"], b + 1)
                act.copy(v1[:, b, :, 0:C], bank[1][:, 0:HW].rearrange("p (s c) -> p s c", s=S)).then_inc(s["v1_ok"], 1)

            def exp_image(b):
                act.wait_ge(s["nmax1_ok"], b + 1)
                if b >= 2:
                    act.wait_ge(s["p1t1_mm"], b - 1)
                for t in range(S):
                    act.activation(p1[:, b % 2, t], bank[5 + b % 2][:, t * HW:(t + 1) * HW], ACT.Exp,
                                   bias=nmax1[:, 2 * b + t:2 * b + t + 1]).then_inc(s["p1_ok"], 1)

            def probs_image(b, tiles=range(S)):
                for t in tiles:
                    probs_out(act.copy, act, b, t)

            value_copy(0)
            exp_image(0)
            value_copy(1)
            probs_image(0)
            exp_image(1)
            value_copy(2)
            probs_image(1)
            exp_image(2)
            value_copy(3)
            probs_image(2, [0])
            exp_image(3)
            probs_image(3, [0])

        @block.vector
        def _(dve):
            qv = q_conv[:, :].rearrange("c (n b x) -> c n b x", b=B, x=R * OW)

            def project_images(g):
                dve.wait_ge(s["qbias_ok"], 1)
                for b in range(G * g, G * g + G):
                    dve.wait_ge(s["q_mm"], max(b + 1, 2))
                    dve.scalar_tensor_tensor(
                        out=qv[:, :, b], in0=query_image(b).rearrange("c (n x) -> c n x", x=R * OW), scalar=w("ln_g"),
                        in1=q_bias[:, :].rearrange("c (n x) -> c n x", x=R * OW),
                        op0=ALU.mult, op1=ALU.add).then_inc(s["q_out"], 1)

            for h in range(2):
                for i in range(4 * h, 4 * h + 4):
                    if i in (0, 2, 4):
                        dve.wait_ge(s[f"x_in{i // 2}"], 16)
                    dve.bn_stats(st[:, i], x_hw[:, i]).then_inc(s["stats"], 1)
                for i in range(4 * h, 4 * h + 4):
                    dve.wait_ge(s["stats"], i + 1)
                    dve.bn_aggr(mv[:, i], st[:, i]).then_inc(s["aggr"], 1)
                if h == 1:
                    dve.wait_ge(s["early_in"], 16)
                    for i in DVE_D:
                        dve.tensor_scalar(diag[:, i, :], w("ident"), tap_weight(PE_TAPS[i]), None, ALU.mult).then_inc(s["diag_v"], 1)
                dve.wait_ge(s["sdev"], h + 1)
                dve.reciprocal(rstd[:, halves(h)], sd[:, halves(h)]).then_inc(s["rstd_ok"], 1)
                dve.wait_ge(s["rstd_ok"], h + 1)
                if h == 0:
                    for i in range(4):
                        dve.tensor_scalar(x_hat[:, i], x_hw[:, i], mv[:, i, 0:1], rstd[:, i:i + 1], ALU.subtract, ALU.mult).then_inc(s["hat_ok"], 1)
                    dve.wait_ge(s["colsum_mm"], 1)
                    dve.tensor_copy(colsum[:, :], bank[5][0:1, 0:C]).then_inc(s["colsum_ok"], 1)
                else:
                    dve.scalar_tensor_tensor(out=shift[:, :], in0=mv[:, halves(1), 0], scalar=-1.0, in1=rstd[:, halves(1)],
                                             op0=ALU.mult, op1=ALU.mult).then_inc(s["shift_ok"], 1)
                    for i in range(4, 6):
                        dve.tensor_scalar(x_hat[:, i], x_hw[:, i], mv[:, i, 0:1], rstd[:, i:i + 1], ALU.subtract, ALU.mult).then_inc(s["hat_ok"], 1)
            project_images(0)
            project_images(1)
            dve.wait_ge(s["q_out"], B)
            for n, tap in enumerate(DVE_TAPS):
                chain, k = n % 2, n // 2
                src, dst = tap_views(tap, acc[:, chain, :])
                if k == 0:
                    ins = dve.tensor_scalar(dst, src, tap_weight(tap), None, ALU.mult)
                else:
                    dve.wait_ge(s[f"acc{chain}_ok"], k)
                    ins = dve.scalar_tensor_tensor(out=dst, in0=src, scalar=tap_weight(tap), in1=dst, op0=ALU.mult, op1=ALU.add)
                ins.then_inc(s[f"acc{chain}_ok"], 1)
            gx, gy = w("grid_x"), w("grid_y").rearrange("p (s q) -> p s q", s=S)
            scale = (H / R) / 2 * 0.5 * (W - 1)

            def rows_apart(g):
                dve.wait_ge(s["tanh_ok"], g + 1)
                dve.wait_ge(s["mid_in"], 16)
                dve.scalar_tensor_tensor(out=dist_y[:, g], in0=tanh[:, g, 1].unsqueeze(1).to_broadcast([P, S, G * PIX]), scalar=scale,
                                         in1=gy, op0=ALU.mult, op1=ALU.add).then_inc(s["dy_ok"], 1)

            def sample_weights(g):
                dve.scalar_tensor_tensor(out=dist_x[:, g], in0=tanh[:, g, 0], scalar=scale,
                                         in1=gx, op0=ALU.mult, op1=ALU.add).then_inc(s["dx_ok"], 1)
                dve.wait_ge(s["dx_ok"], g + 1)
                dve.tensor_scalar(falling_x[:, g], dist_x[:, g], -1.0, 1.0, ALU.mult, ALU.add).then_inc(s["fx_ok"], 1)
                dve.wait_ge(s["fx_ok"], g + 1)
                dve.scalar_tensor_tensor(out=hat_x[:, g], in0=dist_x[:, g], scalar=1.0,
                                         in1=falling_x[:, g], op0=ALU.add, op1=ALU.min).then_inc(s["hx_ok"], 1)

            def bilinear(g):
                dve.wait_ge(s["hx_ok"], g + 1)
                dve.wait_ge(s["hy_ok"], g + 1)
                dve.scalar_tensor_tensor(out=bilin[:, g], in0=hat_x[:, g].unsqueeze(1).to_broadcast([P, S, G * PIX]), scalar=0.0,
                                         in1=hat_y[:, g], op0=ALU.max, op1=ALU.mult).then_inc(s["bilin_ok"], 1)

            def sample_out(g):
                dve.wait_ge(s["interp_mm"], g + 1)
                dve.tensor_copy(sampled[:, 2 * g:2 * g + 2, :].rearrange("p b t -> p (b t)"), bank[g][:, 0:G * PIX]).then_inc(s["sampled_ok"], 1)

            rows_apart(0)
            sample_weights(0)
            rows_apart(1)
            bilinear(0)
            sample_weights(1)
            sample_out(0)
            bilinear(1)
            dve.wait_ge(s["k_mm"], 1)
            dve.wait_ge(s["cols_ok"], 3)
            for b in range(G):
                dve.scalar_tensor_tensor(out=k_blk[:, b], in0=bank[2][:, b * PIX:(b + 1) * PIX].unsqueeze(1).to_broadcast([P, NH, PIX]),
                                         scalar=cols[:, 1:2], in1=w("head_of").unsqueeze(2).to_broadcast([P, NH, PIX]),
                                         op0=ALU.add, op1=ALU.mult).then_inc(s["kblk_ok"], 1)
                if b == 0:
                    sample_out(1)
                    value_half(dve.tensor_copy, dve, 0, 0, s["v_even"])

            def scores(i):
                return bank[3 + i % 2][:, :].rearrange("p (h q) -> p h q", h=NH)

            def max_tile(i):
                dve.wait_ge(s["s_mm"], i + 1)
                dve.tensor_reduce(smax[:, i % 2], scores(i), AX.X, ALU.max).then_inc(s["smax_ok"], 1)

            def shift_tile(i):
                dve.wait_ge(s["smax_ok"], i + 1)
                if i >= 2:
                    dve.wait_ge(s["pt_mm"], i - 1)
                dve.tensor_tensor(s_sub[:, i % 2], scores(i), smax[:, i % 2].unsqueeze(2).to_broadcast([P, NH, PIX]),
                                  ALU.subtract).then_inc(s["ssub_ok"], 1)

            def av(i):
                return bank[5 + i % 2][:, 0:PAIRS * VW].rearrange("p (j d) -> p j d", d=VW)

            def recip_tile(i):
                dve.wait_ge(s["av_mm"], i + 1)
                dve.reciprocal(recip[:, i % 2].rearrange("p (j e) -> p j e", e=2), av(i)[:, :, 2 * HD:VW]).then_inc(s["recip_ok"], 1)

            def norm_tile(i):
                dve.wait_ge(s["recip_ok"], i + 1)
                if i >= 2:
                    dve.wait_ge(s["attt_mm"], i - 1)
                dve.tensor_tensor(att[:, i % 2].rearrange("p (j e d) -> p j e d", j=PAIRS, e=2),
                                  av(i)[:, :, 0:2 * HD].rearrange("p j (e d) -> p j e d", e=2),
                                  recip[:, i % 2].rearrange("p (j e) -> p j e", e=2).unsqueeze(3).to_broadcast([P, PAIRS, 2, HD]),
                                  ALU.mult).then_inc(s["att_ok"], 1)

            def z_tile(i):
                dve.wait_ge(s["msa_mm"], i + 1)
                dve.wait_ge(s["xres_ok"], 1)
                dve.tensor_tensor(z[:, i], bank[1][:, 0:C], x_res[:, i], ALU.add).then_inc(s["z_ok"], 1)

            def z_stats(i):
                dve.wait_ge(s["z_ok"], i + 1)
                dve.bn_stats(zst[:, i], z[:, i]).then_inc(s["zst_ok"], 1)

            def z_aggr(i):
                dve.wait_ge(s["zst_ok"], i + 1)
                dve.bn_aggr(zmv[:, i], zst[:, i]).then_inc(s["zmv_ok"], 1)

            def z_var(b):
                dve.wait_ge(s["zmv_ok"], 2 * b + 2)
                dve.tensor_scalar(zve[:, 2 * b:2 * b + 2], zmv[:, 2 * b:2 * b + 2, 1], LN_EPS, None, ALU.add).then_inc(s["zve_ok"], 1)

            def zhat_image(b):
                dve.wait_ge(s["zrs_ok"], b + 1)
                for i in (2 * b, 2 * b + 1):
                    dve.tensor_scalar(z_hat[:, i], z[:, i], zmv[:, i, 0:1], zrs[:, i:i + 1], ALU.subtract, ALU.mult).then_inc(s["zhat_ok"], 1)

            def x1_image(b):
                dve.wait_ge(s["gel_ok"], b + 1)
                dve.tensor_tensor(x1_t[:, b], gel_t[:, b], zt_bank(b)[:, HW:2 * HW], ALU.add).then_inc(s["x1t_ok"], 1)

            def x1_residual(b):
                dve.wait_ge(s["gelt_mm"], b + 1)
                dve.wait_ge(s["zres_ok"], b + 1)
                dve.tensor_tensor(x1_res[:, 2 * b:2 * b + 2], bank[3 + b][:, HW:2 * HW].rearrange("p (s c) -> p s c", s=S),
                                  z_res[:, 2 * b:2 * b + 2], ALU.add).then_inc(s["x1res_ok"], 1)

            max_tile(0)
            shift_tile(0)
            for i in range(T - 1):
                max_tile(i + 1)
                if i >= 3:
                    z_stats(i - 3)
                shift_tile(i + 1)
                if i >= 3:
                    z_aggr(i - 3)
                if i == 0:
                    value_half(dve.tensor_copy, dve, 0, 1, s["v_even"])
                if i >= 1:
                    recip_tile(i - 1)
                if i >= 2:
                    z_tile(i - 2)
                if i >= 1:
                    norm_tile(i - 1)
                if i >= 4 and i % 2 == 0:
                    z_var((i - 4) // 2)
                if i >= 5 and i % 2 == 1:
                    zhat_image((i - 5) // 2)

            def gn_stats(b):
                dve.wait_ge(s["x1t_ok"], b + 1)
                dve.bn_stats(gst[:, b], x1_t[:, b]).then_inc(s["gst_ok"], 1)

            def gn_aggr(b):
                dve.wait_ge(s["gst_ok"], b + 1)
                dve.bn_aggr(gmv[:, b], gst[:, b]).then_inc(s["gmv_ok"], 1)

            def gn_square(n):
                dve.wait_ge(s["dev_mm"], n + 1)
                for b in GN_SETS[n]:
                    dve.tensor_scalar(dev2[:, b:b + 1], bank[0][:, b:b + 1], bank[0][:, b:b + 1], None, ALU.mult).then_inc(s["dev2_ok"], 1)

            def gn_var(n):
                i = slice(GN_SETS[n].start, GN_SETS[n].stop)
                dve.wait_ge(s["gvar_mm"], n + 1)
                dve.tensor_scalar(gve[:, i], bank[0][:, B + i.start:B + i.stop], GN_EPS, None, ALU.add).then_inc(s["gve_ok"], 1)
                dve.tensor_copy(gmean[:, i], bank[0][:, 2 * B + i.start:2 * B + i.stop]).then_inc(s["gmean_ok"], 1)

            def norm_image(b):
                n = b // 2
                dve.wait_ge(s["gmean_ok"], n + 1)
                dve.wait_ge(s["grs_ok"], n + 1)
                dve.tensor_scalar(x_gn[:, b], x1_t[:, b], gmean[:, b:b + 1], grs[:, b:b + 1],
                                  ALU.subtract, ALU.mult).then_inc(s["xgn_ok"], 1)

            def project_out(b):
                dve.wait_ge(s["qk_mm"], b + 1)
                dve.wait_ge(s["cols1_ok"], 3)
                dve.tensor_scalar(q1[:, b], bank[3 + b % 2][:, 0:HW], cols1[:, 0:1], C ** -0.5, ALU.add, ALU.mult).then_inc(s["q1_ok"], 1)
                dve.tensor_scalar(k1[:, b], bank[3 + b % 2][:, HW:2 * HW], cols1[:, 1:2], None, ALU.add).then_inc(s["k1_ok"], 1)

            def max_image(b):
                t = slice(2 * b, 2 * b + 2)
                dve.wait_ge(s["s1_mm"], b + 1)
                dve.tensor_reduce(nmax1[:, t], bank[5 + b % 2][:, :].rearrange("p (t m) -> p t m", t=2), AX.X, ALU.max,
                                  negate=True).then_inc(s["nmax1_ok"], 1)

            def finish_tile(b, t):
                i = 2 * b + t
                dve.wait_ge(s["x1res_ok"], b + 1)
                dve.wait_ge(s["av1_mm"], i + 1 if b >= 2 else 2 * b + 2)
                dve.reciprocal(rec1[:, i:i + 1], av_bank(b, t)[:, t * HW + C:t * HW + C + 1]).then_inc(s["rec1_ok"], 1)
                dve.wait_ge(s["rec1_ok"], i + 1)
                dve.scalar_tensor_tensor(out=y[:, i], in0=av_bank(b, t)[:, t * HW:t * HW + C], scalar=rec1[:, i:i + 1], in1=x1_res[:, i],
                                         op0=ALU.mult, op1=ALU.add).then_inc(s["y_ok"], 1)

            def finish_image(b):
                for t in range(S):
                    finish_tile(b, t)

            z_stats(T - 4)
            zhat_image(1)
            recip_tile(T - 2)
            norm_tile(T - 2)
            z_aggr(T - 4)
            z_tile(T - 3)
            z_stats(T - 3)
            recip_tile(T - 1)
            norm_tile(T - 1)
            z_aggr(T - 3)
            z_var(2)
            x1_image(0)
            z_tile(T - 2)
            x1_image(1)
            gn_stats(0)
            gn_stats(1)
            z_tile(T - 1)
            gn_aggr(0)
            gn_aggr(1)
            z_stats(T - 2)
            z_stats(T - 1)
            z_aggr(T - 2)
            z_aggr(T - 1)
            z_var(3)
            gn_square(0)
            zhat_image(2)
            x1_residual(0)
            gn_var(0)
            zhat_image(3)
            norm_image(0)
            norm_image(1)
            x1_residual(1)
            x1_image(2)
            gn_stats(2)
            project_out(0)
            x1_residual(2)
            x1_image(3)
            gn_stats(3)
            gn_aggr(2)
            gn_aggr(3)
            x1_residual(3)
            gn_square(1)
            project_out(1)
            gn_var(1)
            max_image(0)
            norm_image(2)
            norm_image(3)
            max_image(1)
            project_out(2)
            finish_image(0)
            max_image(2)
            project_out(3)
            finish_image(1)
            max_image(3)
            probs_out(dve.tensor_copy, dve, 2, 1)
            finish_tile(2, 0)
            probs_out(dve.tensor_copy, dve, 3, 1)
            finish_tile(2, 1)
            finish_image(3)

        @block.tensor
        def _(pe):
            def mm(o, l, r_, start=True, stop=True, **k):
                return pe.matmul(o, l, r_, start=start, stop=stop, **k)

            def keep_warm(n, at=4):
                for _ in range(n):
                    mm(bank[at][:, :], warm[:, :], warm[:, :].unsqueeze(1).to_broadcast([P, 4, P]))

            pe.wait_ge(s["warm_set"], 1)
            keep_warm(N_WARM)
            pe.wait_ge(s["ones_set"], 1)
            pe.wait_ge(s["early_in"], 16)
            mm(bank[5][0:1, 0:C], ones_col[:, :], w("wq_conv")).then_inc(s["colsum_mm"], 1)
            keep_warm(2)
            for i in range(T):
                b, t = divmod(i, S)
                if i == 3:
                    pe.wait_ge(s["colsum_ok"], 1)
                    pe.wait_ge(s["rows_in"], 16)
                    mm(bank[5][:, 0:C], r("ln_b"), colsum[:, :], stop=False)
                    mm(bank[5][:, 0:C], ones_row[:, :], r("bq_conv"), start=False).then_inc(s["qbias_mm"], 1)
                if i == 4:
                    pe.wait_ge(s["fold_in"], 16)
                    mm(bank[6][:, 0:C], w("wqT"), w("mq_w"))
                    mm(bank[6][:, C:C + 1], w("mq_w"), w("bq"))
                    mm(bank[6][:, C + 1:C + 2], w("mk_w"), w("bv"))
                    mm(bank[6][:, C + 2:C + 3], w("mv_w"), w("bv")).then_inc(s["foldq_mm"], 1)
                    keep_warm(1)
                if i < 6:
                    pe.wait_ge(s["hat_ok"], i + 1)
                else:
                    pe.wait_ge(s["hat_a"], i - 5)
                o = query_image(b).rearrange("c (r s n) -> c r s n", r=2, s=S)[:, :, t]
                m = mm(o, x_hat[:, i], w("wq_conv"))
                if t == S - 1:
                    m.then_inc(s["q_mm"], 1)

            a0 = PLACE["fold"][0]["mk_w"][0]
            mm(bank[7][:, 0:2 * C], w("wvT"), packs["fold"][:, a0:a0 + 2 * C]).then_inc(s["foldkv_mm"], 1)

            def query_half(h):
                pe.wait_ge(s["m_q_ok"], 1)
                pe.wait_ge(s["xln_ok"], h + 1)
                mm(bank[4 + h][:, :], m_q[:, :], x_ln[:, halves(h), :].rearrange("p t c -> p (t c)")).then_inc(s["qh_mm"], 1)

            pe.wait_ge(s["q_out"], B)
            for n, tap in enumerate(PE_TAPS):
                for which, done in ((ACT_D, "diag_a"), (DVE_D, "diag_v"), (POOL_D, "diag_p")):
                    if n in which:
                        pe.wait_ge(s[done], which.index(n) + 1)
                src, dst = tap_views(tap, bank[3][:, 0:B * PIX])
                mm(dst, diag[:, n, :], src, start=(n == 0), stop=False, skip_group_check=True)
            for k, done, n in ((3, "accp1_ok", len(POOL_TAPS) // 2), (2, "accp0_ok", (len(POOL_TAPS) - 1) // 2),
                               (1, "acc1_ok", len(DVE_TAPS) // 2), (0, "acc0_ok", (len(DVE_TAPS) + 1) // 2)):
                pe.wait_ge(s[done], n)
                m = mm(bank[3][:, 0:B * PIX], w("ident"), acc[:, k, :], start=False, stop=(k == 0), skip_group_check=True)
            m.then_inc(s["conv_mm"], 1)

            pe.wait_ge(s["gelu_ok"], 1)
            pe.wait_ge(s["m_kv_ok"], 1)
            for g in range(2):
                for d in range(2):
                    m = mm(bank[7 - g][:, d * G * PIX:(d + 1) * G * PIX], w("pw")[:, 1 - d:2 - d].to_broadcast([P, P]),
                           o_act[:, 2 * g:2 * g + 2].rearrange("c b y x -> c (b y x)"))
                m.then_inc(s["coord_mm"], 1)
            query_half(0)
            query_half(1)
            pe.wait_ge(s["cols_ok"], 3)
            pe.wait_ge(s["mid_in"], 16)
            pe.wait_ge(s["tanh_ok"], 2)
            mm(bank[6][:, 0:C], cols[:, 2:3].to_broadcast([P, P]), w("mo_w"), stop=False)
            mm(bank[6][:, 0:C], ones_row[:, :], r("mo_b"), start=False).then_inc(s["msabias_mm"], 1)

            def sample_half(g):
                pe.wait_ge(s["bilin_ok"], g + 1)
                for b in range(G):
                    for t in range(S):
                        for e in range(2):
                            m = mm(bank[g][e * PIX:(e + 1) * PIX, b * PIX:(b + 1) * PIX], bilin[:, g, t, b * PIX:(b + 1) * PIX],
                                   x_hw[:, 2 * (G * g + b) + t].rearrange("p (t e) -> p t e", e=2)[:, :, e],
                                   start=(t == 0), stop=(t == S - 1))
                m.then_inc(s["interp_mm"], 1)

            def key_half(g):
                pe.wait_ge(s["sampled_ok"], g + 1)
                if g == 1:
                    pe.wait_ge(s["kblk_ok"], G)
                mm(bank[2][:, 0:G * PIX], m_kv[:, 0:C], sampled[:, 2 * g:2 * g + 2, :].rearrange("p b t -> p (b t)")).then_inc(s["k_mm"], 1)
                for b in range(G):
                    for e in range(2):
                        m = mm(bank[g][e * PIX:(e + 1) * PIX, b * PIX:(b + 1) * PIX], sampled[:, G * g + b],
                               m_kv[:, C:2 * C].rearrange("p (j e d) -> p j e d", j=PAIRS, e=2)[:, :, e])
                m.then_inc(s["v_mm"], 1)

            sample_half(0)
            pe.wait_ge(s["late_in"], 16)
            mm(bank[7][:, 0:C], w("wv1T"), w("wo1"))
            mm(bank[7][:, C:C + 1], w("wq1"), w("gn_beta"))
            mm(bank[7][:, C + 1:C + 2], w("wk1"), w("gn_beta"))
            mm(bank[7][:, C + 2:C + 3], w("mlp_w"), w("ln_b")).then_inc(s["fold1_mm"], 1)
            key_half(0)
            sample_half(1)

            def score_tile(i):
                b = i // S
                if b < G:
                    pe.wait_ge(s["kblk_ok"], b + 1)
                else:
                    pe.wait_ge(s["kblk_p"], b - G + 1)
                if i % 4 == 0:
                    pe.wait_ge(s["qh_ok"], i // 4 + 1)
                if i >= 2:
                    pe.wait_ge(s["ssub_ok"], i - 1)
                mm(bank[3 + i % 2][:, :], qh[:, i * P:(i + 1) * P], k_blk[:, b].rearrange("p h q -> p (h q)")).then_inc(s["s_mm"], 1)

            def transpose_scores(i):
                pe.wait_ge(s["ssub_ok"], i + 1)
                if i == 0:
                    pe.wait_ge(s["qh_ok"], 2)
                if i == 1:
                    pe.wait_ge(s["msabias_ok"], 1)
                if i >= 2:
                    pe.wait_ge(s["att_ok"], i - 1)
                for j in range(PAIRS):
                    m = pe.transpose(bank[5 + i % 2][:, j * P:(j + 1) * P],
                                     s_sub[:, i % 2, 2 * j:2 * j + 2].rearrange("p h q -> p (h q)"), w("ident"))
                m.then_inc(s["pt_mm"], 1)

            def value_tile(i):
                b = i // S
                pe.wait_ge(s["exp_ok"], i + 1)
                pe.wait_ge(s["v_even"], b // G + 1)
                pe.wait_ge(s["v_odd"], b // G + 1)
                for j in range(PAIRS):
                    m = mm(bank[5 + i % 2][:, j * VW:(j + 1) * VW], p_t[:, i % 2, j], v_blk[:, b, j])
                m.then_inc(s["av_mm"], 1)

            def att_transpose(i):
                pe.wait_ge(s["att_ok"], i + 1)
                if i >= 1:
                    pe.wait_ge(s["attt_ok"], i)
                pe.transpose(bank[0][:, 0:P], att[:, i % 2], w("ident")).then_inc(s["attt_mm"], 1)

            def out_project(i):
                pe.wait_ge(s["attt_ok"], i + 1)
                if i >= 1:
                    pe.wait_ge(s["z_ok"], i)
                mm(bank[1][:, 0:C], att_t[:, i % 2], w("mo_w")).then_inc(s["msa_mm"], 1)

            def z_transpose(b):
                pe.wait_ge(s["z_ok"], 2 * b + 2)
                if b == 0:
                    pe.wait_ge(s["k_ok"], 1)
                elif b == 1:
                    pe.wait_ge(s["outbias_ok"], 1)
                else:
                    pe.wait_ge(s["x1t_ok"], b - 1)
                for t in range(S):
                    pe.transpose(zt_bank(b)[:, HW + t * P:HW + (t + 1) * P], z[:, 2 * b + t], w("ident"))
                pe.wait_ge(s["zhat_ok"], 2 * b + 2)
                for t in range(S):
                    m = pe.transpose(zt_bank(b)[:, t * P:(t + 1) * P], z_hat[:, 2 * b + t], w("ident"))
                m.then_inc(s["zt_mm"], 1)

            def mlp_image(b):
                pe.wait_ge(s["zt_ok"], b + 1)
                pe.wait_ge(s["mlpw_ok"], 1)
                if b < 2:
                    pe.wait_ge(s["ssub_ok"], T - 1 + b)
                else:
                    pe.wait_ge(s["att_ok"], T)
                mm(bank[3 + b][:, 0:HW], mlp_wg[:, :], z_t[:, 2 * b:2 * b + 2, :].rearrange("c s q -> c (s q)")).then_inc(s["mlp_mm"], 1)

            score_tile(0)
            score_tile(1)
            key_half(1)
            for i in range(T - 1):
                transpose_scores(i)
                if i >= 1:
                    value_tile(i - 1)
                if i >= 2:
                    out_project(i - 2)
                if i + 2 < T:
                    score_tile(i + 2)
                    if i >= 1:
                        att_transpose(i - 1)

            def gelu_transpose(b):
                pe.wait_ge(s["gel_ok"], b + 1)
                for t in range(S):
                    m = pe.transpose(bank[3 + b][:, HW + t * P:HW + (t + 1) * P], gel_t[:, b, t * P:(t + 1) * P], w("ident"))
                m.then_inc(s["gelt_mm"], 1)

            def gn_mean(n):
                i = slice(GN_SETS[n].start, GN_SETS[n].stop)
                pe.wait_ge(s["gmv_ok"], i.stop)
                if n == 0:
                    pe.wait_ge(s["attt_ok"], T)
                else:
                    pe.wait_ge(s["gmean_ok"], n)
                mm(bank[0][:, i], w("group_rest"), gmv[:, i, 0]).then_inc(s["dev_mm"], 1)

            def gn_spread(n):
                i = slice(GN_SETS[n].start, GN_SETS[n].stop)
                variance = bank[0][:, B + i.start:B + i.stop]
                pe.wait_ge(s["dev2_ok"], i.stop)
                mm(variance, w("group_mean"), gmv[:, i, 1], stop=False)
                mm(variance, w("group_mean"), dev2[:, i], start=False)
                mm(bank[0][:, 2 * B + i.start:2 * B + i.stop], w("group_mean"), gmv[:, i, 0]).then_inc(s["gvar_mm"], 1)

            def project_qk(b):
                pe.wait_ge(s["xgn_ok"], b + 1)
                pe.wait_ge(s["gamma_ok"], 1)
                if b < 2:
                    pe.wait_ge(s["x1res_ok"], b + 1)
                else:
                    pe.wait_ge(s["k1_ok"], b - 1)
                mm(bank[3 + b % 2][:, 0:HW], wq1g[:, :], x_gn[:, b])
                mm(bank[3 + b % 2][:, HW:2 * HW], wk1g[:, :], x_gn[:, b]).then_inc(s["qk_mm"], 1)

            def project_v(b):
                if b == 0:
                    pe.wait_ge(s["z_ok"], T)
                else:
                    pe.wait_ge(s["v1_ok"], b)
                for t in range(S):
                    m = mm(bank[1][:, t * C:(t + 1) * C], x_gn[:, b, t * P:(t + 1) * P], w_vog[:, :])
                m.then_inc(s["v1_mm"], 1)

            def score_image(b):
                pe.wait_ge(s["q1_ok"], b + 1)
                pe.wait_ge(s["k1_ok"], b + 1)
                if b < 2:
                    pe.wait_ge(s["x1res_ok"], b + 3)
                else:
                    pe.wait_ge(s["p1_ok"], 2 * (b - 1))
                for t in range(S):
                    m = mm(bank[5 + b % 2][:, t * HW:(t + 1) * HW], q1[:, b, t * P:(t + 1) * P], k1[:, b])
                m.then_inc(s["s1_mm"], 1)

            def transpose_tile(b, t):
                pe.wait_ge(s["p1_ok"], 2 * b + t + 1)
                if b >= 1:
                    pe.wait_ge(s[f"p1t{t}_ok"], b)
                elif t == 0:
                    pe.wait_ge(s["x1t_ok"], 3)
                else:
                    pe.wait_ge(s["gmean_ok"], 2)
                for j in range(S):
                    m = pe.transpose(bank[(2, 0)[t]][:, j * P:(j + 1) * P], p1[:, b % 2, t, j * P:(j + 1) * P], w("ident"))
                m.then_inc(s[f"p1t{t}_mm"], 1)

            def transpose_image(b):
                for t in range(S):
                    transpose_tile(b, t)

            def value_rows(b, t):
                pe.wait_ge(s["v1_ok"], b + 1)
                pe.wait_ge(s["v1ones_set"], 1)
                pe.wait_ge(s[f"p1t{t}_ok"], b + 1)
                if (b, t) == (0, 0):
                    pe.wait_ge(s["x1t_ok"], B)
                elif t == 0 and b < 3:
                    pe.wait_ge(s["y_ok"], 2 * b)
                elif b == 3:
                    pe.wait_ge(s["k1_ok"], 3 + t)
                elif b == 2:
                    pe.wait_ge(s["v1_ok"], B)
                for j in range(S):
                    m = mm(av_bank(b, t)[:, t * HW:t * HW + C + 1], p1_t[:, b % 2, t, j], v1[:, b, j], start=(j == 0), stop=(j == S - 1))
                m.then_inc(s["av1_mm"], 1)

            def value_image(b):
                for t in range(S):
                    value_rows(b, t)

            z_transpose(0)
            pe.wait_ge(s["w_vo_ok"], 1)
            pe.wait_ge(s["cols1_ok"], 3)
            mm(bank[7][:, 0:C], w("bv1").to_broadcast([P, P]), w("wo1"), stop=False)
            mm(bank[7][:, 0:C], w("gn_beta").to_broadcast([P, P]), w_vo[:, :], start=False, stop=False)
            mm(bank[7][:, 0:C], ones_row[:, :], r("bo1"), start=False).then_inc(s["outbias_mm"], 1)
            transpose_scores(T - 1)
            att_transpose(T - 3)
            value_tile(T - 2)
            out_project(T - 3)
            z_transpose(1)
            value_tile(T - 1)
            att_transpose(T - 2)
            mlp_image(0)
            mlp_image(1)
            out_project(T - 2)
            att_transpose(T - 1)
            keep_warm(2, 6)
            out_project(T - 1)
            gelu_transpose(0)
            gelu_transpose(1)
            keep_warm(2, 6)
            gn_mean(0)
            keep_warm(2, 6)
            gn_spread(0)
            z_transpose(2)
            z_transpose(3)
            mlp_image(2)
            project_qk(0)
            mlp_image(3)
            gelu_transpose(2)
            project_v(0)
            gelu_transpose(3)
            project_qk(1)
            gn_mean(1)
            score_image(0)
            gn_spread(1)
            project_v(1)
            score_image(1)
            transpose_image(0)
            project_qk(2)
            value_image(0)
            project_v(2)
            score_image(2)
            transpose_image(1)
            project_qk(3)
            value_image(1)
            project_v(3)
            score_image(3)
            transpose_image(2)
            value_rows(2, 0)
            transpose_tile(3, 0)
            value_rows(2, 1)
            transpose_tile(3, 1)
            value_image(3)


def kernel(**inputs):
    import numpy as np
    import concourse.bacc as bacc
    from concourse.bass_utils import run_bass_kernel_spmd as run

    get = {k: np.asarray(v) for k, v in inputs.items()}
    L0, L1 = "L0_conv_", "L1_conv_"
    p = np.arange(P)
    f32 = np.float32

    const = {
        "ident": np.eye(P, dtype=f32),
        "head_of": (p[:, None] // HD == np.arange(NH)[None, :]).astype(f32),
        "ones_mask": (p[:, None] // PIX == np.arange(2)[None, :]).astype(f32),
        "group_rest": (np.eye(P) - (p[:, None] // GROUP == p[None, :] // GROUP) / GROUP).astype(f32),
        "group_mean": ((p[:, None] // GROUP == p[None, :] // GROUP) / GROUP).astype(f32),
    }
    half = np.arange(OH) + 0.5
    centre = ((half * (2.0 / OH)) * (H / R) / 2.0 + 1.0) * 0.5 * (W - 1)
    const["grid_x"] = (np.tile(centre, G * OH)[None, :] - (p % W)[:, None]).astype(f32)
    const["grid_y"] = np.concatenate([np.tile(np.repeat(centre, OW), G)[None, :] - (t * (P // W) + p // W)[:, None]
                                      for t in range(S)], axis=1).astype(f32)

    col = lambda a: a.reshape(C, 1)
    conv_order = lambda a: a.reshape(-1, OH // 2, 2, OW, 2).transpose(0, 2, 1, 4, 3).reshape(-1, C)
    data = {
        "dw_w": get[L0 + "dw_w"].reshape(C, KS * KS), "pw": get[L0 + "pw_w"].reshape(2, C).T,
        "wq_conv": conv_order(get[L0 + "wq"]), "wqT": get[L0 + "wq"].T, "wvT": get[L0 + "wv"].T,
        "wv1T": get[L1 + "wv"].T, "wo1": get[L1 + "wo"], "wq1": get[L1 + "wq"], "wk1": get[L1 + "wk"],
        "bq1": col(get[L1 + "bq"]), "bk1": col(get[L1 + "bk"]), "bv1": col(get[L1 + "bv"]),
        "gn_gamma": col(get[L1 + "gn_gamma"]), "gn_beta": col(get[L1 + "gn_beta"]),
    }
    for n in ("dw_b", "bq", "mq_b", "bv", "mk_b", "mv_b", "ln_g", "ln_b", "mlp_b"):
        data[n] = col(get[L0 + n])
    for n in ("mq_w", "mk_w", "mv_w", "mo_w", "mlp_w"):
        data[n] = get[L0 + n]
    row = {"ln_b": get[L0 + "ln_b"].reshape(1, C), "bq_conv": conv_order(get[L0 + "bq"].reshape(1, C)), "mo_b": get[L0 + "mo_b"].reshape(1, C),
           "bo1": get[L1 + "bo"].reshape(1, C)}

    arrays = {
        "x": np.ascontiguousarray(get["x"]).reshape(B, HW, C),
        **{pack: np.ascontiguousarray(np.concatenate([const[n] if n in const else data[n] for n, _ in parts], axis=1))
           for pack, parts in PACKS.items()},
        "rows": np.ascontiguousarray(np.concatenate([row[n] for n in ROWS], axis=1)),
        "ln_rows": np.ascontiguousarray(np.concatenate([get[L0 + "ln_g"], get[L0 + "ln_b"]])),
    }
    nc = bacc.Bacc("TRN2", target_bir_lowering=False, num_devices=1)
    args = [nc.dram_tensor(n, a.shape, mybir.dt.from_np(a.dtype), kind="ExternalInput").ap() for n, a in arrays.items()]
    out = nc.dram_tensor("out", (B, HW, C), F32, kind="ExternalOutput").ap()
    build(nc, *args, out)
    got = run(nc, [arrays], core_ids=[0]).results[0]["out"]
    return got.reshape(B, H, W, C)
```
